# Optimizing a Trainium2 kernel written in Bass

```python
import numpy as np
import jax
import jax.numpy as jnp

def _softmax(x, axis=-1):
    return jax.nn.softmax(x, axis=axis)

def _gelu(x):
    return jax.nn.gelu(x, approximate=True)

def _silu(x):
    return jax.nn.silu(x)

def _sigmoid(x):
    return jax.nn.sigmoid(x)

def _layernorm(x, axis=-1, eps=1e-05):
    m = jnp.mean(x, axis=axis, keepdims=True)
    v = jnp.var(x, axis=axis, keepdims=True)
    return (x - m) / jnp.sqrt(v + eps)

def _scatter_add(tgt, idx, src, axis=0):
    return tgt.at[idx].add(src)

def _segment_sum(src, seg, n):
    return jax.ops.segment_sum(src, seg, n)
kernel_name = 'mk_prb_d1_jaxref_r8_7c9216'

def setup_inputs(seed: int=0):
    np.random.seed(seed)
    _w = jnp.asarray

    def _L0_attn_setup():
        import jax, jax.numpy as jnp
        import numpy as np
        B, S, E, H = (2, 256, 256, 16)
        D = E // H
        ROPE_BASE = 10000.0

        def rotate_half(x):
            x1 = x[..., ::2]
            x2 = x[..., 1::2]
            return jnp.stack((-x2, x1), axis=-1).reshape(x.shape[:-1] + (x.shape[-1],))

        def rope_cos_sin(seq_len, head_dim, start_pos=0):
            inv_freq = 1.0 / ROPE_BASE ** (jnp.arange(0, head_dim, 2, dtype=jnp.float32) / head_dim)
            positions = jnp.arange(start_pos, start_pos + seq_len, dtype=jnp.float32)
            freqs = jnp.outer(positions, inv_freq)
            emb = jnp.concatenate([freqs, freqs], axis=-1)
            return (emb[None, None].astype(jnp.float32), emb)
        key = jax.random.key(seed)
        k1, k2, k3 = jax.random.split(key, 3)
        x = jax.random.normal(k1, (B, S, E), dtype=jnp.float32)
        Wqkv = jax.random.normal(k2, (3 * E, E), dtype=jnp.float32) * E ** (-0.5)
        Wout = jax.random.normal(k3, (E, E), dtype=jnp.float32) * E ** (-0.5)
        return {'x': x, 'Wqkv': Wqkv, 'Wout': Wout}
    _L0_attn_in = _L0_attn_setup()

    def _L0_ffn_setup():
        import jax, jax.numpy as jnp
        import numpy as np
        B, S, DIM = (4, 64, 256)
        E, INTER = (32, 128)
        G, TOPK_G, TOPK = (8, 4, 6)
        ROUTE_SCALE = 2.5
        SHARED_INTER = 2 * INTER

        def _gate(xf, gate_w):
            scores = jax.nn.sigmoid(xf @ gate_w.T)
            gs = scores.reshape(-1, G, E // G)
            group_scores = gs.max(axis=-1)
            _, gidx = jax.lax.top_k(group_scores, TOPK_G)
            gmask = jnp.any(jnp.arange(G)[None, None, :] == gidx[:, :, None], axis=1)
            masked = jnp.where(gmask[:, :, None], gs, -jnp.inf).reshape(-1, E)
            _, idx = jax.lax.top_k(masked, TOPK)
            w = jnp.take_along_axis(scores, idx, axis=1)
            w = w / jnp.sum(w, axis=-1, keepdims=True) * ROUTE_SCALE
            return (w, idx)
        key = jax.random.key(seed)
        ks = jax.random.split(key, 8)
        sd = 0.02
        return {'x': jax.random.normal(ks[0], (B, S, DIM), jnp.float32), 'gate_w': jax.random.normal(ks[1], (E, DIM), jnp.float32) * sd, 'w11': jax.random.normal(ks[2], (E, INTER, DIM), jnp.float32) * sd, 'w33': jax.random.normal(ks[3], (E, INTER, DIM), jnp.float32) * sd, 'w22': jax.random.normal(ks[4], (E, DIM, INTER), jnp.float32) * sd, 'sw1': jax.random.normal(ks[5], (SHARED_INTER, DIM), jnp.float32) * sd, 'sw2': jax.random.normal(ks[6], (DIM, SHARED_INTER), jnp.float32) * sd, 'sw3': jax.random.normal(ks[7], (SHARED_INTER, DIM), jnp.float32) * sd}
    _L0_ffn_in = _L0_ffn_setup()
    _d = {'L0_attn_x': _L0_attn_in['x'], 'L0_attn_Wqkv': _L0_attn_in['Wqkv'], 'L0_attn_Wout': _L0_attn_in['Wout'], 'L0_ffn_gate_w': _L0_ffn_in['gate_w'], 'L0_ffn_w11': _L0_ffn_in['w11'], 'L0_ffn_w33': _L0_ffn_in['w33'], 'L0_ffn_w22': _L0_ffn_in['w22'], 'L0_ffn_sw1': _L0_ffn_in['sw1'], 'L0_ffn_sw2': _L0_ffn_in['sw2'], 'L0_ffn_sw3': _L0_ffn_in['sw3']}
    _x0 = _d['L0_attn_x']
    _d['L0_attn_x'] = jax.random.normal(jax.random.fold_in(jax.random.key(seed), 1), (1, 2048, 256), dtype=_x0.dtype)
    del _x0
    return _d

def reference(L0_attn_x, L0_attn_Wqkv, L0_attn_Wout, L0_ffn_gate_w, L0_ffn_w11, L0_ffn_w33, L0_ffn_w22, L0_ffn_sw1, L0_ffn_sw2, L0_ffn_sw3):

    def _L0_attn_ref(x, Wqkv, Wout):
        import jax, jax.numpy as jnp
        import numpy as np
        B, S, E, H = (2, 256, 256, 16)
        D = E // H
        ROPE_BASE = 10000.0

        def rotate_half(x):
            x1 = x[..., ::2]
            x2 = x[..., 1::2]
            return jnp.stack((-x2, x1), axis=-1).reshape(x.shape[:-1] + (x.shape[-1],))

        def rope_cos_sin(seq_len, head_dim, start_pos=0):
            inv_freq = 1.0 / ROPE_BASE ** (jnp.arange(0, head_dim, 2, dtype=jnp.float32) / head_dim)
            positions = jnp.arange(start_pos, start_pos + seq_len, dtype=jnp.float32)
            freqs = jnp.outer(positions, inv_freq)
            emb = jnp.concatenate([freqs, freqs], axis=-1)
            return (emb[None, None].astype(jnp.float32), emb)
        batch, seq_len, emb = x.shape
        scale = D ** (-0.5)
        qkv = x @ Wqkv.T
        qkv = qkv.reshape(batch, seq_len, 3, H, D)
        qkv = jnp.transpose(qkv, (2, 0, 3, 1, 4))
        q, k, v = (qkv[0], qkv[1], qkv[2])
        inv_freq = 1.0 / ROPE_BASE ** (jnp.arange(0, D, 2, dtype=jnp.float32) / D)
        positions = jnp.arange(seq_len, dtype=jnp.float32)
        freqs = jnp.outer(positions, inv_freq)
        emb_ang = jnp.concatenate([freqs, freqs], axis=-1)
        cos = jnp.cos(emb_ang)[None, None]
        sin = jnp.sin(emb_ang)[None, None]
        q = q * cos + rotate_half(q) * sin
        k = k * cos + rotate_half(k) * sin
        scores = jnp.einsum('bhqd,bhkd->bhqk', q, k) * scale
        causal = jnp.arange(seq_len)[None, :] > jnp.arange(seq_len)[:, None]
        scores = jnp.where(causal[None, None], -jnp.inf, scores)
        attn = jax.nn.softmax(scores, axis=-1)
        out = jnp.einsum('bhqk,bhkd->bhqd', attn, v)
        out = jnp.transpose(out, (0, 2, 1, 3)).reshape(batch, seq_len, emb)
        return out @ Wout.T

    def _L0_ffn_ref(x, gate_w, w11, w33, w22, sw1, sw2, sw3):
        import jax, jax.numpy as jnp
        import numpy as np
        B, S, DIM = (4, 64, 256)
        E, INTER = (32, 128)
        G, TOPK_G, TOPK = (8, 4, 6)
        ROUTE_SCALE = 2.5
        SHARED_INTER = 2 * INTER

        def _gate(xf, gate_w):
            scores = jax.nn.sigmoid(xf @ gate_w.T)
            gs = scores.reshape(-1, G, E // G)
            group_scores = gs.max(axis=-1)
            _, gidx = jax.lax.top_k(group_scores, TOPK_G)
            gmask = jnp.any(jnp.arange(G)[None, None, :] == gidx[:, :, None], axis=1)
            masked = jnp.where(gmask[:, :, None], gs, -jnp.inf).reshape(-1, E)
            _, idx = jax.lax.top_k(masked, TOPK)
            w = jnp.take_along_axis(scores, idx, axis=1)
            w = w / jnp.sum(w, axis=-1, keepdims=True) * ROUTE_SCALE
            return (w, idx)
        xf = x.reshape(-1, DIM)
        T = xf.shape[0]
        w, idx = _gate(xf, gate_w)
        c = jnp.zeros((T, E), xf.dtype).at[jnp.arange(T)[:, None], idx].add(w)
        g = jnp.einsum('td,eid->tei', xf, w11)
        u = jnp.einsum('td,eid->tei', xf, w33)
        act = jax.nn.silu(g) * u
        y = jnp.einsum('tei,te,edi->td', act, c, w22)
        shared = jax.nn.silu(xf @ sw1.T) * (xf @ sw3.T) @ sw2.T
        return (y + shared).reshape(x.shape)
    x = L0_attn_x
    xn = _layernorm(x, axis=-1)
    x = x + _L0_attn_ref(xn, L0_attn_Wqkv, L0_attn_Wout) + _L0_ffn_ref(xn, L0_ffn_gate_w, L0_ffn_w11, L0_ffn_w33, L0_ffn_w22, L0_ffn_sw1, L0_ffn_sw2, L0_ffn_sw3)
    return x

_drawn_inputs = setup_inputs


def setup_inputs(seed=0):
    import zlib

    import numpy as np

    out = dict(_drawn_inputs(seed))
    spreads = {}
    factors = {'L0_ffn_gate_w': 5.798,
     'L0_ffn_w11': 5.267,
     'L0_ffn_w33': 5.205,
     'L0_ffn_w22': 5.219,
     'L0_ffn_sw1': 3.82,
     'L0_ffn_sw2': 3.806,
     'L0_ffn_sw3': 3.792}
    for name, (base, spread) in spreads.items():
        noise = np.random.default_rng([zlib.crc32(name.encode()), seed]).standard_normal(out[name].shape)
        drawn = base * np.exp(spread * noise) if base else spread * noise
        out[name] = jnp.asarray(drawn.astype(out[name].dtype))
    for name, factor in factors.items():
        out[name] = (out[name] * factor).astype(out[name].dtype)
    return out
```

```python
from contextlib import ExitStack

import numpy as np
import concourse.bass as bass
from concourse import mybir

ALU = mybir.AluOpType
ACT = mybir.ActivationFunctionType
AX = mybir.AxisListType
F32 = mybir.dt.float32
BF16 = mybir.dt.bfloat16
I32 = mybir.dt.int32
U32 = mybir.dt.uint32

P = 128
T = 2048
NT = T // P
D = 256
DC = D // P
H = 16
DH = D // H
HG = 4
NG = H // HG
GW = HG * DH
E = 32
INTER = 128
G = 8
EG = E // G
TOPK_G = 4
TOPK = 6
ROUTE_SCALE = 2.5
EPS = 1e-5
SLOT_TILES = T * TOPK // P + E
SLOTS = SLOT_TILES * P
ATTN_SCALE = DH ** -0.5
TERMS = 6
KQ = TERMS * DH
KM = KQ + 3
CH = 512
NCH = T // CH
TPC = CH // P
NB = 8
VW = 32
MASKED = -1e30
SATURATED = 16.6355
GONE = -1e30
SENTINEL = 1e38
PICKED = 2e38

C_QK, C_V, C_G, C_U, C_L = 0, 2 * D, 3 * D, 4 * D, 5 * D
C_END = C_L + E

MX_UNITS = sum(HG * TPC * (c + 1) for c in range(NCH))
KB_UNITS = sum(TPC * (c + 1) for c in range(NCH))
ST_UNITS = 2 * KB_UNITS
MISC_USES = 3 * NCH


def attention_order():
    mx = {c: [("mx", c, t, j, p) for t in range(TPC * c, TPC * c + TPC) for j in range(HG) for p in range(c + 1)]
          for c in range(NCH)}
    order = mx[0] + [("mt", 0)]
    for c in range(NCH):
        nkb = TPC * (c + 1)
        fill = mx.get(c + 1, [])
        done = 0
        for kb in range(nkb):
            order.append(("st", c, kb))
            upto = len(fill) * (kb + 1) // nkb
            order += fill[done:upto]
            done = upto
            if kb:
                order.append(("pv", c, kb - 1))
            if kb == 1 and c:
                order.append(("ot", c - 1))
        order.append(("pv", c, nkb - 1))
        order.append(("oe", c))
        if c + 1 < NCH:
            order.append(("mt", c + 1))
    order.append(("ot", NCH - 1))
    return order


def layer(nc, x, wqkvT, sw1T, sw3T, gateT, sw2T, woutT, wexp, cos, sin, out):
    xg_dram = nc.dram_tensor("gathered_rows", [SLOTS, D], F32, kind="Internal").ap()
    yg_dram = nc.dram_tensor("expert_rows", [SLOTS, D], F32, kind="Internal").ap()
    order = attention_order()

    with ExitStack() as ctx:
        def sb(name, shape, dt=F32):
            return ctx.enter_context(nc.sbuf_tensor(name, shape, dt))

        def sem(name):
            return ctx.enter_context(nc.semaphore(name))

        bank = [ctx.enter_context(nc.psum_tensor(f"bank{i}", [P, 512], F32)) for i in range(2)]
        st2 = [ctx.enter_context(nc.psum_tensor(f"score_banks{i}", [P, 2, 512], F32)) for i in range(2)]
        bank += [st2[0][:, 0, :], st2[0][:, 1, :], st2[1][:, 0, :], st2[1][:, 1, :]]
        bank += [ctx.enter_context(nc.psum_tensor(f"bank{i}", [P, 512], F32)) for i in (6, 7)]

        def carve(region, words):
            at = 0

            def take(shape, dt=F32):
                nonlocal at
                n = int(np.prod(shape[1:])) * (4 if dt != BF16 else 2) // 4
                part = region[0:shape[0], at:at + n]
                at += n
                assert at <= words
                if dt != F32:
                    part = part.bitcast(dt)
                if len(shape) == 3:
                    part = part.rearrange("p (a b) -> p a b", b=shape[2])
                elif len(shape) == 4:
                    part = part.rearrange("p (a b c) -> p a b c", b=shape[2], c=shape[3])
                return part
            return take

        turned = sb("turned", [P, HG * T])
        probs = sb("probs", [P, 4 * 2 * CH])
        before = carve(turned, HG * T)
        after = carve(turned, HG * T)
        before_probs = carve(probs, 4 * 2 * CH)

        res = sb("res", [P, NT, D])
        xn_all = sb("xn_all", [P, NT, D])
        qk_all = sb("qk_all", [P, NT, 2 * D])
        v_all = sb("v_all", [P, NT, D])
        o_all = sb("o_all", [P, NT, D])
        ident = sb("ident", [P, P])
        identb = sb("identb", [P, P], BF16)
        wcat = before_probs([P, DC, C_END])
        wout = sb("wout", [P, DC, D])
        sw2 = sb("sw2", [P, DC, D])
        cos_sb = before([P, NT, 2 * DH])
        sin_sb = before([P, NT, 2 * DH])
        stat = before([P, NT, 6])
        mv = sb("mv", [P, NT, 2])
        var = sb("var", [P, NT])
        root = sb("root", [P, NT])
        rstd = sb("rstd", [P, NT])
        newton = sb("newton", [P, NT])
        mark = sb("mark", [P, 1])
        xnb = [sb(f"xnb{b}", [P, D]) for b in range(2)]
        xT = [sb(f"xT{b}", [P, DC, P]) for b in range(2)]
        rope_c = before([P, 2 * D])
        rope_s = before([P, 2 * D])
        th = [before([P, D]) for b in range(2)]
        g1 = [before([P, D]) for b in range(2)]
        u1 = [before([P, D]) for b in range(2)]
        hm = [before([P, D]) for b in range(2)]
        hb = [before([P, D]) for b in range(2)]
        hT = [sb(f"hT{b}", [P, DC, P]) for b in range(2)]
        logit = sb("logit", [P, NT, E])
        sig = sb("sig", [P, NT, E])
        key = sb("key", [P, NT, E])
        gx = sb("gx", [P, NT, G + TOPK_G])
        ex = before_probs([P, NT, E + 8 - TOPK])
        top = sb("top", [P, NT, 8])
        pick = before_probs([P, NT, E])
        pickb = sb("pickb", [P, NT, E], BF16)
        wgt = sb("wgt", [P, NT, E])
        wsum = sb("wsum", [P, NT])
        triu = sb("triu", [P, P], BF16)
        onesb = sb("onesb", [P, P], BF16)
        ones_e = sb("ones_e", [P, E])
        cnt = sb("cnt", [P, E], I32)
        pad = sb("pad", [P, E])
        ends = sb("ends", [P, E])
        tile_at = sb("tile_at", [P, 1])
        tile_i = sb("tile_i", [P, 1], I32)
        owner = sb("owner", [P, 1])
        owner_cmp = sb("owner_cmp", [P, E])
        owner_row = sb("owner_row", [1, P], I32)
        slot = sb("slot", [P, NT, 8])
        slot_i = sb("slot_i", [P, NT, TOPK], U32)
        c6 = sb("c6", [P, NT, TOPK])
        cat = [sb(f"cat{i}", [P, NT, HG, KQ], BF16) for i in range(2)]
        rem = sb("rem", [P, NT, HG, DH])
        QT = turned[:, 0:HG * T // 2].bitcast(BF16).rearrange("p (h t) -> p h t", t=T)
        KT = turned[:, HG * T // 2:].bitcast(BF16).rearrange("p (h t) -> p h t", t=T)
        V4 = sb("V4", [P, NT, HG, VW])
        PT = [probs[:, i * 2 * CH:(i + 1) * 2 * CH].rearrange("p (h q) -> p h q", q=CH) for i in range(4)]
        mask_q = sb("mask_q", [P, P], BF16)
        mask_k = sb("mask_k", [P, P], BF16)
        mpart = sb("mpart", [P, TPC, HG, NCH])
        mneg = sb("mneg", [P, TPC * HG])
        mrem = sb("mrem", [P, TPC * HG])
        mcat = sb("mcat", [P, TPC * HG, 3], BF16)
        oT = sb("oT", [P, CH])
        rden = sb("rden", [P, TPC, HG])
        wt = [cat[b // 4][:, (b % 4) * 4:(b % 4) * 4 + 4, :, :].rearrange("p a b c -> p (a b c)").bitcast(F32)
              for b in range(NB)]
        xg = [after([P, D]) for b in range(NB)]
        xgT = [after([P, DC, P]) for b in range(2)]
        eth = [after([P, INTER]) for b in range(2)]
        em = [after([P, INTER]) for b in range(2)]
        eh = [after([P, INTER]) for b in range(2)]
        ehT = [after([P, P]) for b in range(2)]
        ysb = [after([P, D]) for b in range(4)]
        otb = [xnb[b] for b in range(2)]
        otT = [xT[b] for b in range(2)]
        yg = [after([P, TOPK, D]) for b in range(2)]

        names = """x_in w_in zeroed ident_made v4_pad kt_ones rows_kept
            var_ready root_ready xn_ready xn_kept xT_psum xT_ready proj_done rope_done proj_read act_ready hT_psum hT_ready
            shared_done shared_added
            sig_exp pick_ready ranks_done rank_read owner_ready owner_psum owner_row_ready slots_ready
            parts_ready qT_psum qT_ready kT_psum kT_ready v4_ready mx_done mx_read
            misc_done misc_read mcat_ready st_done exp_done pv_done o_read
            scattered exp_x_psum exp_x_ready gu_done gate_ready exp_h_ready exp_hT_psum exp_hT_ready
            y_done y_read ot_ready otT_psum otT_ready outp_done outp_free parts_free v4_free ot_free ysb_free combined written""".split()
        s = {n: sem(n) for n in names}
        tile_in = [sem(f"tile_in{b}") for b in range(NB)]
        y_stored = [sem(f"y_stored{b}") for b in range(4)]
        gathered = [sem(f"gathered{b}") for b in range(2)]
        block = ctx.enter_context(nc.Block())

        @block.sync
        def _(sp):
            sp.dma_start(res[:, :, :], x.rearrange("(t p) d -> p t d", p=P)).then_inc(s["x_in"], 16)
            for dst, src, width in ((C_QK, wqkvT, 3 * D), (C_G, sw1T, D), (C_U, sw3T, D), (C_L, gateT, E)):
                sp.dma_start(wcat[:, :, dst:dst + width],
                             src.rearrange("(c p) n -> p c n", p=P)).then_inc(s["w_in"], 16)
            sp.dma_start(sw2[:, :, :], sw2T.rearrange("(c p) n -> p c n", p=P)).then_inc(s["w_in"], 16)
            sp.dma_start(wout[:, :, :], woutT.rearrange("(c p) n -> p c n", p=P)).then_inc(s["w_in"], 16)
            sp.dma_start(cos_sb[:, :, :], cos.rearrange("(t p) n -> p t n", p=P)).then_inc(s["w_in"], 16)
            sp.dma_start(sin_sb[:, :, :], sin.rearrange("(t p) n -> p t n", p=P)).then_inc(s["w_in"], 16)
            sp.wait_ge(s["v4_pad"], 1)
            zero = V4[:, :, :, :].rearrange("p a b c -> p (a b c)")
            rows = 8 * P
            for n in range(SLOTS // rows):
                sp.dma_start(xg_dram[n * rows:(n + 1) * rows, :].rearrange("(p r) d -> p (r d)", p=P),
                             zero).then_inc(s["zeroed"], 16)

            def load(i, b):
                e = sp.value_load(owner_row[0:1, bass.ds(NB * i + b, 1)], min_val=0, max_val=E - 1)
                sp.dma_start(wt[b], wexp[bass.ds(e, 1), :, :].rearrange("e p n -> (e p) n")).then_inc(tile_in[b], 16)
                sp.dma_start(xg[b][:, :], xg_dram[bass.ds((NB * i + b) * P, P), :]).then_inc(tile_in[b], 16)

            sp.wait_ge(s["owner_row_ready"], 1)
            sp.wait_ge(s["scattered"], 16 * NT * TOPK)
            sp.wait_ge(s["pv_done"], NG * KB_UNITS)
            for b in range(NB):
                load(0, b)
            with sp.Fori(1, SLOT_TILES // NB) as i:
                for b in range(NB):
                    sp.wait_ge(s["y_done"], NB * (i - 1) + b + 1)
                    load(i, b)
            for t in range(NT):
                sp.wait_ge(s["combined"], t + 1)
                sp.dma_start(out[t * P:(t + 1) * P, :], res[:, t, :]).then_inc(s["written"], 16)
            sp.wait_ge(s["written"], 16 * NT)

        @block.gpsimd
        def _(gp):
            gp.memset(V4[:, :, :, :], 0.0).then_inc(s["v4_pad"], 1)
            gp.memset(ident[:, :], 0.0)
            gp.memset(identb[:, :], 0.0)
            gp.memset(mask_q[:, :], 0.0)
            gp.memset(mask_k[:, :], 0.0)
            gp.memset(triu[:, :], 1.0)
            gp.memset(onesb[:, :], 1.0)
            gp.memset(ones_e[:, :], 1.0)
            gp.memset(gx[:, :, G:], SENTINEL)
            gp.memset(ex[:, :, E:], SENTINEL)
            gp.iota(tile_i[:, :], [[0, 1]], base=0, channel_multiplier=P)
            gp.drain()
            for m in (ident, identb):
                gp.affine_select(out=m[:, :], in_=m[:, :], compare_op=ALU.not_equal, fill=1.0, base=0,
                                 pattern=[[-1, P]], channel_multiplier=1)
            gp.affine_select(out=mask_q[:, :], in_=mask_q[:, :], compare_op=ALU.is_ge, fill=MASKED, base=0,
                             pattern=[[-1, P]], channel_multiplier=1)
            gp.affine_select(out=mask_k[:, :], in_=mask_k[:, :], compare_op=ALU.is_ge, fill=MASKED, base=0,
                             pattern=[[1, P]], channel_multiplier=-1)
            gp.affine_select(out=triu[:, :], in_=triu[:, :], compare_op=ALU.is_gt, fill=0.0, base=0,
                             pattern=[[1, P]], channel_multiplier=-1)
            gp.tensor_copy(tile_at[:, :], tile_i[:, :]).then_inc(s["ident_made"], 1)

            def keep(t, b):
                gp.wait_ge(s["xn_ready"], t + 1)
                gp.tensor_copy(xn_all[:, bass.ds(t, 1), :].rearrange("p a n -> p (a n)"), xnb[b][:, :]).then_inc(s["xn_kept"], 1)

            with gp.Fori(0, NT // 2) as i:
                for b in range(2):
                    keep(2 * i + b, b)

            places = (((0, 1, 4), (2, 3), 5), ((0, 2, 5), (1, 3), 4))
            gp.wait_ge(s["rows_kept"], 1)
            gp.drain()
            gp.memset(KT[KQ:KM, :, :], 1.0).then_inc(s["kt_ones"], 1)
            gp.drain()
            with gp.Fori(0, NG) as g:
                gp.wait_ge(s["parts_free"], g + 1)
                for c, (his, mids, lo) in zip(range(2), places):
                    src = qk_all[:, :, bass.ds(g * GW + c * D, GW)].rearrange("p t (h d) -> p t h d", d=DH)

                    def part(n):
                        return cat[c][:, :, :, n * DH:(n + 1) * DH]

                    for n in his:
                        gp.tensor_copy(part(n), src)
                    gp.drain()
                    gp.tensor_tensor(rem[:, :, :, :], src, part(his[0]), ALU.subtract)
                    gp.drain()
                    for n in mids:
                        gp.tensor_copy(part(n), rem[:, :, :, :])
                    gp.drain()
                    last = gp.tensor_tensor(part(lo), rem[:, :, :, :], part(mids[0]), ALU.subtract)
                    gp.drain()
                last.then_inc(s["parts_ready"], 1)
                gp.wait_ge(s["v4_free"], g + 1)
                gp.wait_ge(s["zeroed"], 16 * (SLOTS // (8 * P)))
                gp.tensor_copy(V4[:, :, :, 0:DH],
                               v_all[:, :, bass.ds(g * GW, GW)].rearrange("p t (h d) -> p t h d", d=DH))
                gp.memset(V4[:, :, :, DH:DH + 1], 1.0).then_inc(s["v4_ready"], 1)

            gp.wait_ge(s["slots_ready"], 1)
            for t in range(NT):
                for j in range(TOPK):
                    gp.indirect_dma_start(xg_dram, bass.IndirectOffsetOnAxis(ap=slot_i[:, t, j:j + 1], axis=0),
                                          xn_all[:, t, :], None).then_inc(s["scattered"], 16)

            with gp.Fori(0, NT // 2) as i:
                for b in range(2):
                    t = 2 * i + b
                    gp.wait_ge(s["misc_read"], NG * MISC_USES)
                    gp.wait_ge(s["ot_free"], t + 1)
                    gp.tensor_copy(otb[b][:, :], o_all[:, bass.ds(t, 1), :].rearrange("p a n -> p (a n)")).then_inc(s["ot_ready"], 1)

            def store(i, b, first=False):
                gp.wait_ge(s["y_read"], 4 * i + b + 1)
                gp.dma_start(yg_dram[bass.ds((4 * i + b) * P, P), :], ysb[b][:, :]).then_inc(y_stored[b], 16)

            gp.sem_inc(s["ysb_free"], 4)
            for b in range(4):
                store(0, b)
            with gp.Fori(1, SLOT_TILES // 4) as i:
                for b in range(4):
                    gp.wait_ge(y_stored[b], 16 * i)
                    gp.sem_inc(s["ysb_free"], 1)
                    store(i, b)
            for b in range(4):
                gp.wait_ge(y_stored[b], 16 * (SLOT_TILES // 4))
            for t in range(NT):
                if t >= 2:
                    gp.wait_ge(s["combined"], t - 1)
                for j in range(TOPK):
                    gp.indirect_dma_start(yg[t % 2][:, j, :], None, yg_dram,
                                          bass.IndirectOffsetOnAxis(ap=slot_i[:, t, j:j + 1], axis=0)).then_inc(gathered[t % 2], 16)

        @block.scalar
        def _(act):
            A = nc.scalar.activation

            def copy(dst, src):
                return A(dst, src, ACT.Copy)

            def proj(t, b, early):
                act.wait_ge(s["xT_psum"], t + 1)
                if not early:
                    act.wait_ge(s["proj_done"], t - 1)
                copy(xT[b][:, :, :], bank[0][:, 0:D].rearrange("p (c n) -> p c n", n=P)).then_inc(s["xT_ready"], 1)
                act.wait_ge(s["proj_done"], t + 1)
                if not early:
                    act.wait_ge(s["act_ready"], t - 1)
                A(th[b][:, :], bank[3 + b][:, D:2 * D], ACT.Tanh, scale=0.5)
                copy(g1[b][:, :], bank[3 + b][:, D:2 * D])
                copy(v_all[:, bass.ds(t, 1), :].rearrange("p a n -> p (a n)"), bank[3 + b][:, 0:D])
                copy(u1[b][:, :], bank[5][:, 0:D])
                copy(logit[:, bass.ds(t, 1), :].rearrange("p a n -> p (a n)"), bank[5][:, D:D + E]).then_inc(s["proj_read"], 1)

            def shared(t, b, early):
                act.wait_ge(s["hT_psum"], t + 1)
                if not early:
                    act.wait_ge(s["shared_done"], t - 1)
                copy(hT[b][:, :, :], bank[7][:, 0:D].rearrange("p (c n) -> p c n", n=P)).then_inc(s["hT_ready"], 1)

            act.wait_ge(s["var_ready"], 1)
            A(root[:, :], var[:, :], ACT.Sqrt).then_inc(s["root_ready"], 1)
            proj(0, 0, True)
            proj(1, 1, True)
            shared(0, 0, True)
            proj(2, 0, False)
            shared(1, 1, True)
            proj(3, 1, False)
            shared(2, 0, False)
            with act.Fori(2, NT // 2) as i:
                proj(2 * i, 0, False)
                shared(2 * i - 1, 1, False)
                proj(2 * i + 1, 1, False)
                shared(2 * i, 0, False)
            shared(NT - 1, 1, False)

            act.drain()
            A(sig[:, :, :], logit[:, :, :], ACT.Exp, scale=-1.0).then_inc(s["sig_exp"], 1)

            with act.Fori(0, NG) as g:
                for n in range(2 * HG):
                    j, half = n // 2, n % 2
                    act.wait_ge(s["kT_psum"], g * 8 + n + 1)
                    copy(KT[0:KQ, j, half * 1024:half * 1024 + 1024],
                         bank[2 + n % 2][0:KQ, :].bitcast(BF16)).then_inc(s["kT_ready"], 1)
                v = 0
                for step in order:
                    if step[0] != "st":
                        continue
                    _, c, kb = step
                    w = min(CH, CH - (kb - TPC * c) * P)
                    for half in range(2):
                        act.wait_ge(s["st_done"], g * ST_UNITS + v + 1)
                        if v >= 4:
                            act.wait_ge(s["pv_done"], g * KB_UNITS + v // 2 - 1)
                        A(PT[v % 4][:, :, 0:w], st2[v % 2][:, :, 0:w], ACT.Exp).then_inc(s["exp_done"], 1)
                        v += 1

            with act.Fori(0, NT // 2) as i:
                for b in range(2):
                    t = 2 * i + b
                    act.wait_ge(s["otT_psum"], t + 1)
                    act.wait_ge(s["outp_free"], t + 1)
                    copy(otT[b][:, :, :], bank[b][:, 0:D].rearrange("p (c n) -> p c n", n=P)).then_inc(s["otT_ready"], 1)

            def gate(n, b, early=False):
                act.wait_ge(s["gu_done"], n + 1)
                if not early:
                    act.wait_ge(s["exp_h_ready"], n - 1)
                A(eth[b][:, :], bank[2 + b][:, 0:INTER], ACT.Tanh, scale=0.5).then_inc(s["gate_ready"], 1)

            def turn(n, b, early=False):
                act.wait_ge(s["exp_hT_psum"], n + 1)
                if not early:
                    act.wait_ge(s["y_done"], n - 1)
                copy(ehT[b][:, :], bank[4 + b][:, 0:P]).then_inc(s["exp_hT_ready"], 1)

            def keep_y(n, slot4):
                act.wait_ge(s["y_done"], n + 1)
                act.wait_ge(s["ysb_free"], n + 1)
                copy(ysb[slot4][:, :], bank[6 + slot4 % 2][:, 0:D]).then_inc(s["y_read"], 1)

            gate(0, 0, True)
            gate(1, 1, True)
            turn(0, 0, True)
            gate(2, 0)
            turn(1, 1, True)
            keep_y(0, 0)
            with act.Fori(1, SLOT_TILES // 4) as i:
                for b in range(4):
                    n = 4 * i + b
                    gate(n - 1, (b - 1) % 2)
                    turn(n - 2, b % 2)
                    m = (b - 3) % 4
                    act.wait_ge(s["y_done"], n - 2)
                    act.wait_ge(s["ysb_free"], n - 2)
                    copy(ysb[m][:, :], bank[6 + m % 2][:, 0:D]).then_inc(s["y_read"], 1)
            gate(SLOT_TILES - 1, 1)
            turn(SLOT_TILES - 2, 0)
            keep_y(SLOT_TILES - 3, 1)
            turn(SLOT_TILES - 1, 1)
            keep_y(SLOT_TILES - 2, 2)
            keep_y(SLOT_TILES - 1, 3)

        @block.vector
        def _(dve):
            V = nc.vector

            def norm(t, b, early=False):
                if not early:
                    dve.wait_ge(s["xT_psum"], t - 1)
                    dve.wait_ge(s["xn_kept"], t - 1)
                row = res[:, bass.ds(t, 1), :].rearrange("p a n -> p (a n)")
                V.tensor_scalar(xnb[b][:, :], row, mv[:, bass.ds(t, 1), 0], rstd[:, bass.ds(t, 1)],
                                ALU.subtract, ALU.mult).then_inc(s["xn_ready"], 1)

            def rope(t, b):
                dve.wait_ge(s["proj_done"], t + 1)
                y = bank[1 + b][:, :]
                ct = cos_sb[:, bass.ds(t, 1), :].rearrange("p a (c d) -> p (a c) d", d=DH)
                sn = sin_sb[:, bass.ds(t, 1), :].rearrange("p a (c d) -> p (a c) d", d=DH)
                for c in range(2):
                    yc = y[:, c * D:(c + 1) * D].rearrange("p (h d) -> p h d", d=DH)
                    V.tensor_tensor(rope_c[:, c * D:(c + 1) * D].rearrange("p (h d) -> p h d", d=DH), yc,
                                    ct[:, c, :].unsqueeze(1).to_broadcast([P, H, DH]), ALU.mult)
                    for odd in range(2):
                        last = V.tensor_tensor(
                            rope_s[:, c * D:(c + 1) * D].rearrange("p (h d) -> p h d", d=DH)[:, :, odd::2],
                            yc[:, :, 1 - odd::2],
                            sn[:, c, odd::2].unsqueeze(1).to_broadcast([P, H, DH // 2]), ALU.mult)
                last.then_inc(s["rope_done"], 1)
                dve.drain()
                V.tensor_tensor(qk_all[:, bass.ds(t, 1), :].rearrange("p a n -> p (a n)"), rope_c[:, :], rope_s[:, :], ALU.add)

            def shared_act(t, b, early):
                dve.wait_ge(s["proj_read"], t + 1)
                if not early:
                    dve.wait_ge(s["hT_psum"], t - 1)
                V.scalar_tensor_tensor(out=hm[b][:, :], in0=th[b][:, :], scalar=1.0, in1=g1[b][:, :],
                                       op0=ALU.add, op1=ALU.mult)
                dve.drain()
                V.scalar_tensor_tensor(out=hb[b][:, :], in0=hm[b][:, :], scalar=0.5, in1=u1[b][:, :],
                                       op0=ALU.mult, op1=ALU.mult).then_inc(s["act_ready"], 1)

            def shared_add(t):
                dve.wait_ge(s["shared_done"], t + 1)
                row = res[:, bass.ds(t, 1), :].rearrange("p a n -> p (a n)")
                V.tensor_tensor(row, row, bank[6][:, 0:D], ALU.add).then_inc(s["shared_added"], 1)

            dve.wait_ge(s["x_in"], 16)
            for t in range(NT):
                V.bn_stats(stat[:, t, :], res[:, t, :])
            dve.drain()
            for t in range(NT):
                V.bn_aggr(mv[:, t, :], stat[:, t, :])
            dve.drain()
            V.tensor_scalar(var[:, :], mv[:, :, 1], EPS, None, ALU.add).then_inc(s["var_ready"], 1)
            dve.wait_ge(s["root_ready"], 1)
            V.reciprocal(rstd[:, :], root[:, :])
            dve.drain()
            V.tensor_tensor(newton[:, :], rstd[:, :], rstd[:, :], ALU.mult)
            dve.drain()
            V.tensor_tensor(newton[:, :], newton[:, :], var[:, :], ALU.mult)
            dve.drain()
            V.tensor_scalar(newton[:, :], newton[:, :], -0.5, 1.5, ALU.mult, ALU.add)
            dve.drain()
            V.tensor_tensor(rstd[:, :], rstd[:, :], newton[:, :], ALU.mult)
            dve.drain()
            norm(0, 0, True)
            norm(1, 1, True)
            dve.wait_ge(s["w_in"], 16 * 8)
            rope(0, 0)
            shared_act(0, 0, True)
            norm(2, 0)
            rope(1, 1)
            shared_act(1, 1, True)
            shared_add(0)
            norm(3, 1)
            with dve.Fori(1, NT // 2 - 1) as i:
                for b in range(2):
                    t = 2 * i + b
                    rope(t, b)
                    shared_act(t, b, False)
                    shared_add(t - 1)
                    norm(t + 2, b)
            for t in (NT - 2, NT - 1):
                rope(t, t % 2)
                shared_act(t, t % 2, False)
                shared_add(t - 1)
            shared_add(NT - 1)
            dve.drain()
            V.memset(mark[:, :], 0.0).then_inc(s["rows_kept"], 1)

            dve.wait_ge(s["sig_exp"], 1)
            dve.wait_ge(s["ident_made"], 1)
            V.tensor_scalar(key[:, :, :], logit[:, :, :], SATURATED, None, ALU.min)
            V.tensor_scalar(sig[:, :, :], sig[:, :, :], 1.0, None, ALU.add)
            dve.drain()
            V.tensor_reduce(gx[:, :, 0:G], key[:, :, :].rearrange("p t (g e) -> p t g e", e=EG), AX.X, ALU.max)
            V.reciprocal(sig[:, :, :], sig[:, :, :])
            dve.drain()
            for t in range(NT):
                V.max(out=top[:, t, :], in_=gx[:, t, :])
            dve.drain()
            for t in range(NT):
                V.match_replace(out=gx[:, t, :], in_to_replace=top[:, t, :], in_values=gx[:, t, :], imm_value=PICKED)
            dve.drain()
            V.tensor_scalar(gx[:, :, 0:G], gx[:, :, 0:G], PICKED, GONE, ALU.not_equal, ALU.mult)
            dve.drain()
            V.tensor_tensor(ex[:, :, 0:E].rearrange("p t (g e) -> p t g e", e=EG),
                            key[:, :, :].rearrange("p t (g e) -> p t g e", e=EG),
                            gx[:, :, 0:G].unsqueeze(3).to_broadcast([P, NT, G, EG]), ALU.add)
            dve.drain()
            for t in range(NT):
                V.max(out=top[:, t, :], in_=ex[:, t, :])
            dve.drain()
            for t in range(NT):
                V.match_replace(out=ex[:, t, :], in_to_replace=top[:, t, :], in_values=ex[:, t, :], imm_value=PICKED)
            dve.drain()
            V.tensor_scalar(pickb[:, :, :], ex[:, :, 0:E], PICKED, None, ALU.is_equal).then_inc(s["pick_ready"], 1)
            V.tensor_scalar(pick[:, :, :], ex[:, :, 0:E], PICKED, None, ALU.is_equal)
            dve.drain()
            V.tensor_tensor(wgt[:, :, :], pick[:, :, :], sig[:, :, :], ALU.mult)
            dve.drain()
            V.tensor_reduce(wsum[:, :], wgt[:, :, :], AX.X, ALU.add)
            dve.drain()
            V.reciprocal(wsum[:, :], wsum[:, :])
            dve.drain()
            V.scalar_tensor_tensor(out=wgt[:, :, :], in0=wgt[:, :, :], scalar=ROUTE_SCALE,
                                   in1=wsum[:, :].unsqueeze(2).to_broadcast([P, NT, E]),
                                   op0=ALU.mult, op1=ALU.mult)
            dve.wait_ge(s["ranks_done"], 1)
            V.tensor_scalar(cnt[:, :], bank[1][:, 0:E], float(P - 1), None, ALU.add)
            dve.drain()
            V.tensor_scalar(cnt[:, :], cnt[:, :], P.bit_length() - 1, None, ALU.arith_shift_right)
            dve.drain()
            V.tensor_scalar(pad[:, :], cnt[:, :], float(P), None, ALU.mult)
            dve.drain()
            V.tensor_tensor_scan(ends[:, :], ones_e[:, :], pad[:, :], 0.0, ALU.mult, ALU.add)
            dve.drain()
            V.tensor_tensor(owner_cmp[:, :], ends[:, :], tile_at[:, 0:1].to_broadcast([P, E]), ALU.is_le)
            V.tensor_tensor(pad[:, :], ends[:, :], pad[:, :], ALU.subtract)
            dve.drain()
            V.tensor_reduce(owner[:, :], owner_cmp[:, :], AX.X, ALU.add)
            V.scalar_tensor_tensor(out=key[:, :, :], in0=bank[0][:, :].rearrange("p (t e) -> p t e", e=E), scalar=1.0,
                                   in1=pad[:, :].unsqueeze(1).to_broadcast([P, NT, E]),
                                   op0=ALU.add, op1=ALU.add)
            dve.drain()
            V.tensor_scalar(owner[:, :], owner[:, :], float(E - 1), None, ALU.min).then_inc(s["owner_ready"], 1)
            V.tensor_tensor(key[:, :, :], key[:, :, :], pick[:, :, :], ALU.mult)
            dve.drain()
            for t in range(NT):
                V.max(out=slot[:, t, :], in_=key[:, t, :])
            dve.drain()
            V.tensor_scalar(slot_i[:, :, :], slot[:, :, 0:TOPK], 1.0, None, ALU.subtract).then_inc(s["slots_ready"], 1)
            for j in range(TOPK):
                V.tensor_tensor(sig[:, :, :], key[:, :, :], slot[:, :, j:j + 1].to_broadcast([P, NT, E]), ALU.is_equal)
                dve.drain()
                V.tensor_tensor(sig[:, :, :], sig[:, :, :], wgt[:, :, :], ALU.mult)
                dve.drain()
                V.tensor_reduce(c6[:, :, j], sig[:, :, :], AX.X, ALU.add)
                dve.drain()
            dve.wait_ge(s["owner_psum"], 1)
            V.tensor_copy(owner_row[0:1, :], bank[1][0:1, 256:256 + P]).then_inc(s["owner_row_ready"], 1)

            with dve.Fori(0, NG) as g:
                for n in range(2 * HG):
                    j, half = n // 2, n % 2
                    dve.wait_ge(s["qT_psum"], g * 8 + n + 1)
                    V.tensor_copy(QT[0:KQ, j, half * 1024:half * 1024 + 1024],
                                  bank[n % 2][0:KQ, :].bitcast(BF16)).then_inc(s["qT_ready"], 1)
                u = misc = 0
                for step in order:
                    if step[0] == "mx":
                        _, c, t, j, p = step
                        w = CH if p < c else (t % TPC + 1) * P
                        dve.wait_ge(s["mx_done"], g * MX_UNITS + u + 1)
                        V.tensor_reduce(mpart[:, t % TPC, j, p:p + 1], bank[u % 2][:, 0:w], AX.X,
                                        ALU.max).then_inc(s["mx_read"], 1)
                        u += 1
                    elif step[0] == "mt":
                        c = step[1]
                        dve.drain()
                        V.tensor_reduce(mneg[:, :].rearrange("p (t h) -> p t h", h=HG), mpart[:, :, :, 0:c + 1], AX.X, ALU.max)
                        dve.drain()
                        V.tensor_scalar(mneg[:, :], mneg[:, :], -1.0, None, ALU.mult)
                        dve.drain()
                        V.tensor_copy(mcat[:, :, 0], mneg[:, :])
                        dve.drain()
                        V.tensor_tensor(mrem[:, :], mneg[:, :], mcat[:, :, 0], ALU.subtract)
                        dve.drain()
                        V.tensor_copy(mcat[:, :, 1], mrem[:, :])
                        dve.drain()
                        V.tensor_tensor(mcat[:, :, 2], mrem[:, :], mcat[:, :, 1], ALU.subtract).then_inc(s["mcat_ready"], 1)
                        for pair in range(2):
                            dve.wait_ge(s["misc_done"], g * MISC_USES + misc + 1)
                            V.tensor_copy(QT[KQ:KM, 2 * pair:2 * pair + 2, c * CH:(c + 1) * CH],
                                          bank[7][KQ:KM, :].bitcast(BF16).rearrange("p (h q) -> p h q", q=CH)).then_inc(s["misc_read"], 1)
                            misc += 1
                    elif step[0] == "oe":
                        c = step[1]
                        dve.wait_ge(s["pv_done"], g * KB_UNITS + sum(TPC * (a + 1) for a in range(c + 1)))
                        V.tensor_copy(oT[:, :], bank[6][:, :]).then_inc(s["o_read"], 1)
                    elif step[0] == "ot":
                        c = step[1]
                        dve.wait_ge(s["misc_done"], g * MISC_USES + misc + 1)
                        o4 = bank[7][:, :].rearrange("p (t h v) -> p t h v", t=TPC, h=HG)
                        V.reciprocal(rden[:, :, :], o4[:, :, :, DH])
                        dve.drain()
                        V.tensor_tensor(o_all[:, TPC * c:TPC * (c + 1), bass.ds(g * GW, GW)].rearrange("p t (h d) -> p t h d", d=DH),
                                        o4[:, :, :, 0:DH], rden[:, :, :].unsqueeze(3).to_broadcast([P, TPC, HG, DH]),
                                        ALU.mult).then_inc(s["misc_read"], 1)
                        misc += 1

            dve.sem_inc(s["outp_free"], 2)
            with dve.Fori(0, NT // 2) as i:
                for b in range(2):
                    t = 2 * i + b
                    dve.wait_ge(s["outp_done"], t + 1)
                    row = res[:, bass.ds(t, 1), :].rearrange("p a n -> p (a n)")
                    V.tensor_tensor(row, row, bank[2 + b][:, 0:D], ALU.add).then_inc(s["outp_free"], 1)

            def rows(n, b, early=False):
                dve.wait_ge(s["exp_x_psum"], n + 1)
                if not early:
                    dve.wait_ge(s["gu_done"], n - 1)
                V.tensor_copy(xgT[b][:, :, :], bank[b][:, 0:D].rearrange("p (c n) -> p c n", n=P)).then_inc(s["exp_x_ready"], 1)

            def gated(n, b, early=False):
                dve.wait_ge(s["gate_ready"], n + 1)
                if not early:
                    dve.wait_ge(s["exp_hT_psum"], n - 1)
                V.scalar_tensor_tensor(out=em[b][:, :], in0=eth[b][:, :], scalar=1.0, in1=bank[2 + b][:, 0:INTER],
                                       op0=ALU.add, op1=ALU.mult)
                dve.drain()
                V.scalar_tensor_tensor(out=eh[b][:, :], in0=em[b][:, :], scalar=0.5, in1=bank[2 + b][:, INTER:2 * INTER],
                                       op0=ALU.mult, op1=ALU.mult).then_inc(s["exp_h_ready"], 1)

            rows(0, 0, True)
            rows(1, 1, True)
            gated(0, 0, True)
            rows(2, 0)
            gated(1, 1, True)
            rows(3, 1)
            gated(2, 0)
            with dve.Fori(1, SLOT_TILES // 4) as i:
                for b in range(4):
                    rows(4 * i + b, b % 2)
                    gated(4 * i + b - 1, (b - 1) % 2)
            gated(SLOT_TILES - 1, 1)

            for t in range(NT):
                dve.wait_ge(gathered[t % 2], 16 * TOPK * (t // 2 + 1))
                for j in range(TOPK):
                    dve.drain()
                    last = V.scalar_tensor_tensor(out=res[:, t, :], in0=yg[t % 2][:, j, :], scalar=c6[:, t, j:j + 1],
                                                  in1=res[:, t, :], op0=ALU.mult, op1=ALU.add)
                last.then_inc(s["combined"], 1)

        @block.tensor
        def _(pe):
            mm = nc.tensor.matmul

            def turn(dst, src, eye):
                return nc.tensor.transpose(dst, src, eye)

            def proj(t, b, first=False, early=False):
                pe.wait_ge(s["xn_ready"], t + 1)
                for c in range(DC):
                    last = turn(bank[0][:, c * P:(c + 1) * P], xnb[b][:, c * P:(c + 1) * P], ident[:, :])
                last.then_inc(s["xT_psum"], 1)
                pe.wait_ge(s["xT_ready"], t + 1)
                if not early:
                    pe.wait_ge(s["rope_done"], t - 1)
                if not first:
                    pe.wait_ge(s["proj_read"], t)
                for dst, c0, c1 in ((bank[1 + b], C_QK, C_V), (bank[3 + b], C_V, C_U), (bank[5], C_U, C_END)):
                    for c in range(DC):
                        last = mm(dst[:, 0:c1 - c0], xT[b][:, c, :], wcat[:, c, c0:c1], start=c == 0, stop=c == DC - 1)
                last.then_inc(s["proj_done"], 1)

            def shared(t, b, first=False):
                pe.wait_ge(s["act_ready"], t + 1)
                for c in range(DC):
                    last = turn(bank[7][:, c * P:(c + 1) * P], hb[b][:, c * P:(c + 1) * P], ident[:, :])
                last.then_inc(s["hT_psum"], 1)
                pe.wait_ge(s["hT_ready"], t + 1)
                if not first:
                    pe.wait_ge(s["shared_added"], t)
                for c in range(DC):
                    last = mm(bank[6][:, 0:D], hT[b][:, c, :], sw2[:, c, :], start=c == 0, stop=c == DC - 1)
                last.then_inc(s["shared_done"], 1)

            pe.wait_ge(s["ident_made"], 1)
            pe.wait_ge(s["w_in"], 16 * 8)
            proj(0, 0, True, True)
            proj(1, 1, False, True)
            shared(0, 0, True)
            with pe.Fori(1, NT // 2) as i:
                proj(2 * i, 0)
                shared(2 * i - 1, 1)
                proj(2 * i + 1, 1)
                shared(2 * i, 0)
            shared(NT - 1, 1)

            pe.wait_ge(s["shared_added"], NT)
            pe.wait_ge(s["pick_ready"], 1)
            pk = pickb[:, :, :].rearrange("p t e -> p (t e)")
            mm(bank[0][:, :], triu[:, :], pk, start=True, stop=True, skip_group_check=True)
            for d in range(1, NT):
                mm(bank[0][:, d * E:], onesb[:, :], pk[:, 0:(NT - d) * E], start=False, stop=True, skip_group_check=True)
            for t in range(NT):
                last = mm(bank[1][:, 0:E], onesb[:, :], pickb[:, t, :], start=t == 0, stop=t == NT - 1)
            last.then_inc(s["ranks_done"], 1)
            pe.wait_ge(s["slots_ready"], 1)
            mm(bank[1][0:1, 256:256 + P], owner[:, 0:1], ident[:, :], start=True, stop=True).then_inc(s["owner_psum"], 1)
            pe.wait_ge(s["owner_row_ready"], 1)

            pe.sem_inc(s["parts_free"], 1)
            pe.sem_inc(s["v4_free"], 1)
            with pe.Fori(0, NG) as g:
                pe.wait_ge(s["parts_ready"], g + 1)
                for n in range(2 * HG):
                    j, half = n // 2, n % 2
                    for c, base, psum, ready in ((0, 0, "qT_psum", "qT_ready"), (1, 2, "kT_psum", "kT_ready")):
                        if n >= 2:
                            pe.wait_ge(s[ready], g * 8 + n - 1)
                        dst = bank[base + n % 2][0:KQ, :].bitcast(BF16)
                        for k in range(8):
                            last = turn(dst[:, k * P:(k + 1) * P], cat[c][:, half * 8 + k, j, :], identb[:, :])
                        last.then_inc(s[psum], 1)
                pe.wait_ge(s["qT_ready"], g * 8 + 8)
                pe.wait_ge(s["kT_ready"], g * 8 + 8)
                pe.sem_inc(s["parts_free"], 1)
                pe.wait_ge(s["kt_ones"], 1)
                u = v = n = misc = 0
                for step in order:
                    if step[0] == "mx":
                        _, c, t, j, p = step
                        w = CH if p < c else (t % TPC + 1) * P
                        if u >= 2:
                            pe.wait_ge(s["mx_read"], g * MX_UNITS + u - 1)
                        last = mm(bank[u % 2][:, 0:w], QT[0:KQ, j, t * P:(t + 1) * P], KT[0:KQ, j, p * CH:p * CH + w],
                                  start=True, stop=p < c)
                        if p == c:
                            last = mm(bank[u % 2][:, w - P:w], identb[:, :], mask_q[:, :], start=False, stop=True)
                        last.then_inc(s["mx_done"], 1)
                        u += 1
                    elif step[0] == "mt":
                        c = step[1]
                        pe.wait_ge(s["mcat_ready"], g * NCH + c + 1)
                        for pair in range(2):
                            if misc:
                                pe.wait_ge(s["misc_read"], g * MISC_USES + misc)
                            for j in range(2):
                                for t in range(TPC):
                                    k = j * TPC + t
                                    last = turn(bank[7][KQ:KM, :].bitcast(BF16)[:, k * P:(k + 1) * P],
                                                mcat[:, t * HG + 2 * pair + j, :], identb[:, :])
                            last.then_inc(s["misc_done"], 1)
                            misc += 1
                        pe.wait_ge(s["misc_read"], g * MISC_USES + misc)
                    elif step[0] == "st":
                        _, c, kb = step
                        off = max(0, kb - TPC * c) * P
                        for pair in range(2):
                            if v >= 2:
                                pe.wait_ge(s["exp_done"], g * ST_UNITS + v - 1)
                            for j in range(2):
                                h = 2 * pair + j
                                diag = kb >= TPC * c
                                last = mm(st2[v % 2][:, j, 0:CH - off], KT[0:KM, h, kb * P:(kb + 1) * P],
                                          QT[0:KM, h, c * CH + off:(c + 1) * CH], start=True, stop=not diag)
                                if diag:
                                    last = mm(st2[v % 2][:, j, 0:P], identb[:, :], mask_k[:, :], start=False, stop=True)
                            last.then_inc(s["st_done"], 1)
                            v += 1
                    elif step[0] == "pv":
                        _, c, kb = step
                        off = max(0, kb - TPC * c) * P
                        if n == 0:
                            pe.wait_ge(s["v4_ready"], g + 1)
                        if kb == 0 and c:
                            pe.wait_ge(s["o_read"], g * NCH + c)
                        pe.wait_ge(s["exp_done"], g * ST_UNITS + 2 * n + 2)
                        for h in range(HG):
                            last = mm(bank[6][VW * h:VW * (h + 1), off:CH], V4[:, kb, h, :],
                                      PT[(2 * n + h // 2) % 4][:, h % 2, 0:CH - off],
                                      start=kb == 0, stop=kb == TPC * (c + 1) - 1, skip_group_check=True)
                        last.then_inc(s["pv_done"], 1)
                        n += 1
                    elif step[0] == "ot":
                        c = step[1]
                        pe.wait_ge(s["o_read"], g * NCH + c + 1)
                        pe.wait_ge(s["misc_read"], g * MISC_USES + misc)
                        for t in range(TPC):
                            last = turn(bank[7][:, t * P:(t + 1) * P], oT[:, t * P:(t + 1) * P], ident[:, :])
                        last.then_inc(s["misc_done"], 1)
                        misc += 1
                pe.sem_inc(s["v4_free"], 1)

            pe.wait_ge(s["misc_read"], NG * MISC_USES)
            pe.sem_inc(s["ot_free"], 2)
            with pe.Fori(0, NT // 2) as i:
                for b in range(2):
                    t = 2 * i + b
                    pe.wait_ge(s["ot_ready"], t + 1)
                    pe.wait_ge(s["outp_free"], t + 1)
                    for c in range(DC):
                        last = turn(bank[b][:, c * P:(c + 1) * P], otb[b][:, c * P:(c + 1) * P], ident[:, :])
                    last.then_inc(s["otT_psum"], 1)
                    pe.wait_ge(s["otT_ready"], t + 1)
                    pe.sem_inc(s["ot_free"], 1)
                    for c in range(DC):
                        last = mm(bank[2 + b][:, 0:D], otT[b][:, c, :], wout[:, c, :], start=c == 0, stop=c == DC - 1)
                    last.then_inc(s["outp_done"], 1)
            pe.wait_ge(s["outp_free"], NT + 2)

            def rows(n, b, i, early=False):
                pe.wait_ge(tile_in[b], 32 * i + 32)
                if not early:
                    pe.wait_ge(s["exp_x_ready"], n - 1)
                for c in range(DC):
                    last = turn(bank[b % 2][:, c * P:(c + 1) * P], xg[b][:, c * P:(c + 1) * P], ident[:, :])
                last.then_inc(s["exp_x_psum"], 1)

            def gate_up(n, b, early=False):
                pe.wait_ge(s["exp_x_ready"], n + 1)
                if not early:
                    pe.wait_ge(s["exp_h_ready"], n - 1)
                for c in range(DC):
                    last = mm(bank[2 + b % 2][:, 0:2 * INTER], xgT[b % 2][:, c, :], wt[b][:, c * D:(c + 1) * D],
                              start=c == 0, stop=c == DC - 1)
                last.then_inc(s["gu_done"], 1)

            def hidden(n, b, early=False):
                pe.wait_ge(s["exp_h_ready"], n + 1)
                if not early:
                    pe.wait_ge(s["exp_hT_ready"], n - 1)
                turn(bank[4 + b % 2][:, 0:P], eh[b % 2][:, :], ident[:, :]).then_inc(s["exp_hT_psum"], 1)

            def down(n, b, early=False):
                pe.wait_ge(s["exp_hT_ready"], n + 1)
                if not early:
                    pe.wait_ge(s["y_read"], n - 1)
                mm(bank[6 + b % 2][:, 0:D], ehT[b % 2][:, :], wt[b][:, 2 * D:3 * D], start=True, stop=True).then_inc(s["y_done"], 1)

            rows(0, 0, 0, True)
            rows(1, 1, 0, True)
            gate_up(0, 0, True)
            rows(2, 2, 0)
            gate_up(1, 1, True)
            hidden(0, 0, True)
            rows(3, 3, 0)
            gate_up(2, 2)
            hidden(1, 1, True)
            down(0, 0, True)
            for n in range(4, NB):
                rows(n, n, 0)
                gate_up(n - 1, n - 1)
                hidden(n - 2, n - 2)
                down(n - 3, n - 3)
            with pe.Fori(1, SLOT_TILES // NB) as i:
                for b in range(NB):
                    n = NB * i + b
                    rows(n, b, i)
                    gate_up(n - 1, (b - 1) % NB)
                    hidden(n - 2, (b - 2) % NB)
                    down(n - 3, (b - 3) % NB)
            gate_up(SLOT_TILES - 1, NB - 1)
            hidden(SLOT_TILES - 2, NB - 2)
            down(SLOT_TILES - 3, NB - 3)
            hidden(SLOT_TILES - 1, NB - 1)
            down(SLOT_TILES - 2, NB - 2)
            down(SLOT_TILES - 1, NB - 1)


def rope_tables():
    inv = (np.float32(1.0) / np.float32(10000.0) ** (np.arange(0, DH, 2, dtype=np.float32) / np.float32(DH))).astype(np.float32)
    ang = np.outer(np.arange(T, dtype=np.float32), inv).astype(np.float32)
    ang = np.concatenate([ang, ang], axis=1).astype(np.float64)
    sign = np.where(np.arange(DH) % 2 == 0, -1.0, 1.0)
    c, n = np.cos(ang), np.sin(ang) * sign
    return (np.concatenate([c * ATTN_SCALE, c], 1).astype(np.float32),
            np.concatenate([n * ATTN_SCALE, n], 1).astype(np.float32))


def kernel(L0_attn_x, L0_attn_Wqkv, L0_attn_Wout, L0_ffn_gate_w, L0_ffn_w11, L0_ffn_w33, L0_ffn_w22,
           L0_ffn_sw1, L0_ffn_sw2, L0_ffn_sw3):
    import concourse.bacc as bacc
    from concourse.bass_utils import run_bass_kernel_spmd

    def lay(a):
        return np.ascontiguousarray(a)

    up = np.concatenate([np.asarray(L0_ffn_w11).transpose(0, 2, 1), np.asarray(L0_ffn_w33).transpose(0, 2, 1)], axis=2)
    up = up.reshape(E, DC, P, 2 * INTER).transpose(0, 2, 1, 3).reshape(E, P, DC * 2 * INTER)
    cos, sin = rope_tables()
    arrays = {
        "x": lay(np.asarray(L0_attn_x).reshape(T, D)),
        "wqkvT": lay(np.asarray(L0_attn_Wqkv).T),
        "sw1T": lay(np.asarray(L0_ffn_sw1).T),
        "sw3T": lay(np.asarray(L0_ffn_sw3).T),
        "gateT": lay(np.asarray(L0_ffn_gate_w).T),
        "sw2T": lay(np.asarray(L0_ffn_sw2).T),
        "woutT": lay(np.asarray(L0_attn_Wout).T),
        "wexp": lay(np.concatenate([up, np.asarray(L0_ffn_w22).transpose(0, 2, 1)], axis=2)),
        "cos": cos,
        "sin": sin,
    }
    nc = bacc.Bacc("TRN2", target_bir_lowering=False, num_devices=1)
    args = [nc.dram_tensor(n, a.shape, mybir.dt.from_np(a.dtype), kind="ExternalInput").ap() for n, a in arrays.items()]
    out = nc.dram_tensor("out", [T, D], F32, kind="ExternalOutput").ap()
    layer(nc, *args, out)
    r = run_bass_kernel_spmd(nc, [arrays], core_ids=[0])
    return r.results[0]["out"].reshape(1, T, D)
```

```python
from contextlib import ExitStack

import numpy as np
import concourse.bass as bass
from concourse import mybir

ALU = mybir.AluOpType
ACT = mybir.ActivationFunctionType
AX = mybir.AxisListType
F32 = mybir.dt.float32
BF16 = mybir.dt.bfloat16
I32 = mybir.dt.int32
U32 = mybir.dt.uint32

P = 128
T = 2048
NT = T // P
D = 256
DC = D // P
H = 16
DH = D // H
HG = 4
NG = H // HG
GW = HG * DH
E = 32
INTER = 128
G = 8
EG = E // G
TOPK_G = 4
TOPK = 6
ROUTE_SCALE = 2.5
EPS = 1e-5
SLOT_TILES = T * TOPK // P + E
SLOTS = SLOT_TILES * P
ATTN_SCALE = DH ** -0.5
TERMS = 6
KQ = TERMS * DH
KM = KQ + 3
CH = 512
NCH = T // CH
TPC = CH // P
ZERO_ROWS = NT * GW // D
NB = 8
VW = 32
MASKED = -1e30
SATURATED = 16.6355
GONE = -1e30
SENTINEL = 1e38
PICKED = 2e38

C_QK, C_V, C_G, C_U, C_L = 0, 2 * D, 3 * D, 4 * D, 5 * D
C_END = C_L + E

HALF = NT // 2


def strips(c):
    return [("mx", c, t, j, p) for t in range(TPC * c, TPC * c + TPC) for j in range(HG) for p in range(c + 1)]


def turns(half):
    return [(kind, j, half) for j in range(HG) for kind in ("q", "k")]


def blocks(group, c):
    return [(group, c, kb) for kb in range(TPC * (c + 1))]


def weave(pending, key_blocks, fill, finish=0):
    order, done, later = [], 0, []
    slots = 4 * max(1, len(key_blocks) - finish)
    at = 0

    def some():
        nonlocal done, at
        at += 1
        upto = min(len(fill), -(-len(fill) * at // slots))
        for step in fill[done:upto]:
            order.append(step)
            if step[0] == "mx" and step == strips(step[1])[-1]:
                order.append(("mc", step[1]))
                later.append((at + 2, ("mt", step[1], 0)))
                later.append((at + 4, ("mt", step[1], 1)))
        done = max(done, upto)
        for when, step in [x for x in later if x[0] <= at]:
            order.append(step)
            later.remove((when, step))

    for group, c, kb in key_blocks:
        order.append(("st", group, c, kb, 0))
        some()
        order.append(("st", group, c, kb, 1))
        some()
        if pending:
            order.append(("pv", *pending))
            if pending[2] == TPC * (pending[1] + 1) - 1:
                order.append(("oe", *pending[:2]))
                later.append((at + 3, ("ot", *pending[:2])))
                if pending[1] == NCH - 1:
                    order.append(("v4",))
        some()
        some()
        pending = (group, c, kb)
    for step in fill[done:]:
        order.append(step)
        if step[0] == "mx" and step == strips(step[1])[-1]:
            order.append(("mc", step[1]))
            later += [(0, ("mt", step[1], 0)), (0, ("mt", step[1], 1))]
    order += [step for _, step in later]
    return order, pending


def flush(order, pending):
    return order + [("pv", *pending), ("oe", *pending[:2]), ("ot", *pending[:2])]


def attention_orders():
    first = turns(0) + strips(0) + [("mc", 0), ("mt", 0, 0), ("mt", 0, 1)] + turns(1)
    pending = None
    for c in range(NCH - 1):
        part, pending = weave(pending, blocks(0, c), strips(c + 1))
        first += part
    body, ended = weave(None, blocks(0, NCH - 1) + [b for c in range(NCH - 1) for b in blocks(1, c)],
                        turns(0) + strips(0) + strips(1) + turns(1) + strips(2) + strips(3), finish=2)
    last, left = weave(None, blocks(0, NCH - 1), [])
    return flush(first, pending), flush(body, ended), flush(last, left)


COUNTED = {"ring": ("q", "mx"), "k": ("k",), "st": ("st",), "pv": ("pv",), "mc": ("mc",), "misc": ("mt", "ot"),
           "oe": ("oe",), "v4": ("v4",)}


class Place:

    def __init__(self, *parts):
        self.base = {name: sum(times * sum(step[0] in kinds for step in order) for order, times in parts)
                     for name, kinds in COUNTED.items()}
        self.here = dict.fromkeys(COUNTED, 0)

    def __getitem__(self, name):
        return self.base[name] + self.here[name]

    def passed(self, step):
        for name, kinds in COUNTED.items():
            self.here[name] += step[0] in kinds


def parity(group):
    return group % 2


def layer(nc, x, wqkvT, sw1T, sw3T, gateT, sw2T, woutT, wexp, cos, sin, out):
    xg_dram = nc.dram_tensor("gathered_rows", [SLOTS, D], F32, kind="Internal").ap()
    yg_dram = nc.dram_tensor("expert_rows", [SLOTS, D], F32, kind="Internal").ap()
    first, body, last_part = attention_orders()

    with ExitStack() as ctx:
        def sb(name, shape, dt=F32):
            return ctx.enter_context(nc.sbuf_tensor(name, shape, dt))

        def sem(name):
            return ctx.enter_context(nc.semaphore(name))

        bank = [ctx.enter_context(nc.psum_tensor(f"bank{i}", [P, 512], F32)) for i in range(2)]
        st2 = [ctx.enter_context(nc.psum_tensor(f"score_banks{i}", [P, 2, 512], F32)) for i in range(2)]
        bank += [st2[0][:, 0, :], st2[0][:, 1, :], st2[1][:, 0, :], st2[1][:, 1, :]]
        bank += [ctx.enter_context(nc.psum_tensor(f"bank{i}", [P, 512], F32)) for i in (6, 7)]

        def carve(region, words):
            at = 0

            def take(shape, dt=F32):
                nonlocal at
                n = int(np.prod(shape[1:])) * (4 if dt != BF16 else 2) // 4
                part = region[0:shape[0], at:at + n]
                at += n
                assert at <= words
                if dt != F32:
                    part = part.bitcast(dt)
                if len(shape) == 3:
                    part = part.rearrange("p (a b) -> p a b", b=shape[2])
                elif len(shape) == 4:
                    part = part.rearrange("p (a b c) -> p a b c", b=shape[2], c=shape[3])
                return part
            return take

        turned = sb("turned", [P, 2 * HG * T])
        probs = sb("probs", [P, 4 * 2 * CH])
        before = carve(turned[:, 0:HG * T], HG * T)
        routing = carve(turned[:, HG * T:], HG * T)
        ffn = carve(turned[:, HG * T:], HG * T)
        ending = carve(turned[:, HG * T:], HG * T)
        before_probs = carve(probs, 4 * 2 * CH)
        ffn_probs = carve(probs, 4 * 2 * CH)

        res = sb("res", [P, NT, D])
        xn_all = sb("xn_all", [P, NT, D])
        qk_all = sb("qk_all", [P, NT, 2 * D])
        v_all = sb("v_all", [P, NT, D])
        o_all = v_all
        ident = sb("ident", [P, P])
        identb = sb("identb", [P, P], BF16)
        wcat = before_probs([P, DC, C_END])
        wout = sb("wout", [P, DC, D])
        sw2 = before_probs([P, DC, D])
        cos_sb = before([P, NT, 2 * DH])
        sin_sb = before([P, NT, 2 * DH])
        stat = before([P, NT, 6])
        mv = sb("mv", [P, NT, 2])
        var = sb("var", [P, NT])
        root = sb("root", [P, NT])
        rstd = sb("rstd", [P, NT])
        newton = sb("newton", [P, NT])
        mark = sb("mark", [P, 1])
        xnb = [before([P, D]) for b in range(2)]
        xT = [before([P, DC, P]) for b in range(2)]
        rope_c = before([P, 2 * D])
        rope_s = before([P, 2 * D])
        th = [before([P, D]) for b in range(2)]
        g1 = [before([P, D]) for b in range(2)]
        u1 = [before([P, D]) for b in range(2)]
        hm = [before([P, D]) for b in range(2)]
        hb = [before([P, D]) for b in range(2)]
        hT = [before([P, DC, P]) for b in range(2)]
        logit = routing([P, NT, E])
        sig = routing([P, NT, E])
        key = routing([P, NT, E])
        gx = routing([P, NT, G + TOPK_G])
        ex = routing([P, NT, E + 8 - TOPK])
        top = routing([P, NT, 8])
        pick = routing([P, NT, E])
        pickb = routing([P, NT, E], BF16)
        wgt = routing([P, NT, E])
        wsum = sb("wsum", [P, NT])
        triu = sb("triu", [P, P], BF16)
        onesb = sb("onesb", [P, P], BF16)
        ones_e = sb("ones_e", [P, E])
        cnt = sb("cnt", [P, E], I32)
        pad = sb("pad", [P, E])
        ends = sb("ends", [P, E])
        tile_at = sb("tile_at", [P, 1])
        tile_i = sb("tile_i", [P, 1], I32)
        owner = sb("owner", [P, 1])
        owner_cmp = sb("owner_cmp", [P, E])
        owner_row = sb("owner_row", [1, P], I32)
        slot = routing([P, NT, 8])
        slot_i = sb("slot_i", [P, NT, TOPK], U32)
        c6 = sb("c6", [P, NT, TOPK])
        cat = [sb("cat_q", [P, NT, HG, KQ], BF16), sb("cat_k", [P, NT, HG, KM], BF16)]
        rem = sb("rem", [P, NT, HG, DH])
        QK = turned[:, :].bitcast(BF16)

        def q_turned(par, rows, j, q0, w):
            return QK[rows, bass.ds(par * 2 * HG * T + j * T + q0, w)]

        def k_turned(par, rows, j, k0, w):
            return QK[rows, bass.ds(par * 2 * HG * T + (HG + j) * T + k0, w)]

        V4 = sb("V4", [P, NT, HG, VW])
        PT = [probs[:, i * 2 * CH:(i + 1) * 2 * CH].rearrange("p (h q) -> p h q", q=CH) for i in range(4)]
        mask_q = sb("mask_q", [P, P], BF16)
        mask_k = sb("mask_k", [P, P], BF16)
        mpart = sb("mpart", [P, TPC, HG, NCH])
        mneg = sb("mneg", [P, TPC * HG])
        mrem = sb("mrem", [P, TPC * HG])
        mcat = sb("mcat", [P, TPC * HG, 3], BF16)
        oT = sb("oT", [P, CH])
        rden = sb("rden", [P, TPC, HG])
        wt = [ffn([P, 3 * D]) for b in range(NB)]
        xg = [ffn([P, D]) for b in range(NB)]
        xgT = [ffn_probs([P, DC, P]) for b in range(2)]
        eth = [ffn_probs([P, INTER]) for b in range(2)]
        em = [ffn_probs([P, INTER]) for b in range(2)]
        eh = [ffn_probs([P, INTER]) for b in range(2)]
        ehT = [ffn_probs([P, P]) for b in range(2)]
        ysb = [ffn_probs([P, D]) for b in range(4)]
        otb = [ending([P, D]) for b in range(2)]
        otT = [ending([P, DC, P]) for b in range(2)]
        yg = [xn_all[:, 6 * b:6 * b + 6, :] for b in range(2)]

        names = """x_in w_in zeroed ident_made zeros_made rows_kept
            var_ready root_ready xn_ready xn_kept xT_psum xT_ready proj_done rope_done proj_read act_ready hT_psum hT_ready
            shared_done shared_added
            sig_exp pick_ready ranks_done owner_ready owner_psum owner_row_ready slots_ready attention_done
            parts_ready kT_psum kT_ready v4_ready mx_done mx_read
            misc_done misc_read mcat_ready st_done exp_done pv_done o_read
            scattered exp_x_psum exp_x_ready gu_done gate_ready exp_h_ready exp_hT_psum exp_hT_ready
            y_done y_read ot_ready otT_psum otT_ready outp_done outp_free parts_free ot_free ysb_free combined written""".split()
        s = {n: sem(n) for n in names}
        tile_in = [sem(f"tile_in{b}") for b in range(NB)]
        y_stored = [sem(f"y_stored{b}") for b in range(4)]
        gathered = [sem(f"gathered{b}") for b in range(2)]
        block = ctx.enter_context(nc.Block())

        @block.sync
        def _(sp):
            sp.dma_start(res[:, :, :], x.rearrange("(t p) d -> p t d", p=P)).then_inc(s["x_in"], 16)
            for dst, src, width in ((C_QK, wqkvT, 3 * D), (C_G, sw1T, D), (C_U, sw3T, D), (C_L, gateT, E)):
                sp.dma_start(wcat[:, :, dst:dst + width],
                             src.rearrange("(c p) n -> p c n", p=P)).then_inc(s["w_in"], 16)
            sp.dma_start(sw2[:, :, :], sw2T.rearrange("(c p) n -> p c n", p=P)).then_inc(s["w_in"], 16)
            sp.dma_start(wout[:, :, :], woutT.rearrange("(c p) n -> p c n", p=P)).then_inc(s["w_in"], 16)
            sp.dma_start(cos_sb[:, :, :], cos.rearrange("(t p) n -> p t n", p=P)).then_inc(s["w_in"], 16)
            sp.dma_start(sin_sb[:, :, :], sin.rearrange("(t p) n -> p t n", p=P)).then_inc(s["w_in"], 16)
            sp.wait_ge(s["zeros_made"], 1)
            zero = rem[:, :, :, :].rearrange("p a b c -> p (a b c)")
            rows = ZERO_ROWS * P
            for n in range(SLOTS // rows):
                sp.dma_start(xg_dram[n * rows:(n + 1) * rows, :].rearrange("(p r) d -> p (r d)", p=P),
                             zero).then_inc(s["zeroed"], 16)

            def load(i, b):
                e = sp.value_load(owner_row[0:1, bass.ds(NB * i + b, 1)], min_val=0, max_val=E - 1)
                sp.dma_start(wt[b], wexp[bass.ds(e, 1), :, :].rearrange("e p n -> (e p) n")).then_inc(tile_in[b], 16)
                sp.dma_start(xg[b][:, :], xg_dram[bass.ds((NB * i + b) * P, P), :]).then_inc(tile_in[b], 16)

            sp.wait_ge(s["owner_row_ready"], 1)
            sp.wait_ge(s["scattered"], 16 * NT * TOPK)
            sp.wait_ge(s["pv_done"], Place((first, 1), (body, 1))["pv"] + TPC * NCH)
            for b in range(NB):
                load(0, b)
            with sp.Fori(1, SLOT_TILES // NB) as i:
                for b in range(NB):
                    sp.wait_ge(s["y_done"], NB * (i - 1) + b + 1)
                    load(i, b)
            for t in range(NT):
                sp.wait_ge(s["outp_free"], t + 3)
                sp.dma_start(out[t * P:(t + 1) * P, :], res[:, t, :]).then_inc(s["written"], 16)
            sp.wait_ge(s["written"], 16 * NT)

        @block.gpsimd
        def _(gp):
            gp.memset(rem[:, :, :, :], 0.0).then_inc(s["zeros_made"], 1)
            gp.memset(V4[:, :, :, :], 0.0)
            gp.memset(ident[:, :], 0.0)
            gp.memset(identb[:, :], 0.0)
            gp.memset(mask_q[:, :], 0.0)
            gp.memset(mask_k[:, :], 0.0)
            gp.memset(triu[:, :], 1.0)
            gp.memset(onesb[:, :], 1.0)
            gp.memset(ones_e[:, :], 1.0)
            gp.memset(cat[1][:, :, :, KQ:KM], 1.0)
            gp.memset(gx[:, :, G:], SENTINEL)
            gp.memset(ex[:, :, E:], SENTINEL)
            gp.iota(tile_i[:, :], [[0, 1]], base=0, channel_multiplier=P)
            gp.drain()
            gp.memset(V4[:, :, :, DH:DH + 1], 1.0)
            for m in (ident, identb):
                gp.affine_select(out=m[:, :], in_=m[:, :], compare_op=ALU.not_equal, fill=1.0, base=0,
                                 pattern=[[-1, P]], channel_multiplier=1)
            gp.affine_select(out=mask_q[:, :], in_=mask_q[:, :], compare_op=ALU.is_ge, fill=MASKED, base=0,
                             pattern=[[-1, P]], channel_multiplier=1)
            gp.affine_select(out=mask_k[:, :], in_=mask_k[:, :], compare_op=ALU.is_ge, fill=MASKED, base=0,
                             pattern=[[1, P]], channel_multiplier=-1)
            gp.affine_select(out=triu[:, :], in_=triu[:, :], compare_op=ALU.is_gt, fill=0.0, base=0,
                             pattern=[[1, P]], channel_multiplier=-1)
            gp.tensor_copy(tile_at[:, :], tile_i[:, :]).then_inc(s["ident_made"], 1)

            def keep(t, b):
                gp.wait_ge(s["xn_ready"], t + 1)
                gp.tensor_copy(xn_all[:, bass.ds(t, 1), :].rearrange("p a n -> p (a n)"), xnb[b][:, :]).then_inc(s["xn_kept"], 1)

            with gp.Fori(0, NT // 2) as i:
                for b in range(2):
                    keep(2 * i + b, b)

            places = (((0, 1, 4), (2, 3), 5), ((0, 2, 5), (1, 3), 4))
            def prepare(g):
                gp.wait_ge(s["parts_free"], g + 1)
                for c, (his, mids, lo) in zip(range(2), places):
                    src = qk_all[:, :, bass.ds(g * GW + c * D, GW)].rearrange("p t (h d) -> p t h d", d=DH)

                    def part(n):
                        return cat[c][:, :, :, n * DH:(n + 1) * DH]

                    for n in his:
                        gp.tensor_copy(part(n), src)
                    gp.drain()
                    gp.tensor_tensor(rem[:, :, :, :], src, part(his[0]), ALU.subtract)
                    gp.drain()
                    for n in mids:
                        gp.tensor_copy(part(n), rem[:, :, :, :])
                    gp.drain()
                    last = gp.tensor_tensor(part(lo), rem[:, :, :, :], part(mids[0]), ALU.subtract)
                    gp.drain()
                last.then_inc(s["parts_ready"], 1)

            gp.wait_ge(s["zeroed"], 16 * (SLOTS // (ZERO_ROWS * P)))
            gp.wait_ge(s["rows_kept"], 1)
            with gp.Fori(0, 2) as g:
                prepare(g)

            gp.wait_ge(s["slots_ready"], 1)
            for t in range(NT):
                for j in range(TOPK):
                    gp.indirect_dma_start(xg_dram, bass.IndirectOffsetOnAxis(ap=slot_i[:, t, j:j + 1], axis=0),
                                          xn_all[:, t, :], None).then_inc(s["scattered"], 16)
            with gp.Fori(2, NG) as g:
                prepare(g)

            def store(i, b, first=False):
                gp.wait_ge(s["y_read"], 4 * i + b + 1)
                gp.dma_start(yg_dram[bass.ds((4 * i + b) * P, P), :], ysb[b][:, :]).then_inc(y_stored[b], 16)

            gp.sem_inc(s["ysb_free"], 4)
            for b in range(4):
                store(0, b)
            with gp.Fori(1, SLOT_TILES // 4) as i:
                for b in range(4):
                    gp.wait_ge(y_stored[b], 16 * i)
                    gp.sem_inc(s["ysb_free"], 1)
                    store(i, b)
            for b in range(4):
                gp.wait_ge(y_stored[b], 16 * (SLOT_TILES // 4))
            for t in range(NT):
                if t >= 2:
                    gp.wait_ge(s["combined"], t - 1)
                for j in range(TOPK):
                    gp.indirect_dma_start(yg[t % 2][:, j, :], None, yg_dram,
                                          bass.IndirectOffsetOnAxis(ap=slot_i[:, t, j:j + 1], axis=0)).then_inc(gathered[t % 2], 16)

            gp.wait_ge(s["attention_done"], 1)
            with gp.Fori(0, NT // 2) as i:
                for b in range(2):
                    t = 2 * i + b
                    gp.wait_ge(s["ot_free"], t + 1)
                    gp.tensor_copy(otb[b][:, :], o_all[:, bass.ds(t, 1), :].rearrange("p a n -> p (a n)")).then_inc(s["ot_ready"], 1)


        @block.scalar
        def _(act):
            A = nc.scalar.activation

            def copy(dst, src):
                return A(dst, src, ACT.Copy)

            def proj(t, b, early):
                act.wait_ge(s["xT_psum"], t + 1)
                if not early:
                    act.wait_ge(s["proj_done"], t - 1)
                copy(xT[b][:, :, :], bank[0][:, 0:D].rearrange("p (c n) -> p c n", n=P)).then_inc(s["xT_ready"], 1)
                act.wait_ge(s["proj_done"], t + 1)
                if not early:
                    act.wait_ge(s["act_ready"], t - 1)
                A(th[b][:, :], bank[3 + b][:, D:2 * D], ACT.Tanh, scale=0.5)
                copy(g1[b][:, :], bank[3 + b][:, D:2 * D])
                copy(v_all[:, bass.ds(t, 1), :].rearrange("p a n -> p (a n)"), bank[3 + b][:, 0:D])
                copy(u1[b][:, :], bank[5][:, 0:D])
                copy(logit[:, bass.ds(t, 1), :].rearrange("p a n -> p (a n)"), bank[5][:, D:D + E]).then_inc(s["proj_read"], 1)

            def shared(t, b, early):
                act.wait_ge(s["hT_psum"], t + 1)
                if not early:
                    act.wait_ge(s["shared_done"], t - 1)
                copy(hT[b][:, :, :], bank[7][:, 0:D].rearrange("p (c n) -> p c n", n=P)).then_inc(s["hT_ready"], 1)

            act.wait_ge(s["var_ready"], 1)
            A(root[:, :], var[:, :], ACT.Sqrt).then_inc(s["root_ready"], 1)
            proj(0, 0, True)
            proj(1, 1, True)
            shared(0, 0, True)
            proj(2, 0, False)
            shared(1, 1, True)
            proj(3, 1, False)
            shared(2, 0, False)
            with act.Fori(2, NT // 2) as i:
                proj(2 * i, 0, False)
                shared(2 * i - 1, 1, False)
                proj(2 * i + 1, 1, False)
                shared(2 * i, 0, False)
            shared(NT - 1, 1, False)

            act.drain()
            A(sig[:, :, :], logit[:, :, :], ACT.Exp, scale=-1.0).then_inc(s["sig_exp"], 1)

            def take_v(group):
                copy(V4[:, :, :, 0:DH], v_all[:, :, bass.ds(group * GW, GW)].rearrange("p t (h d) -> p t h d", d=DH)
                     ).then_inc(s["v4_ready"], 1)

            def attend(order, turned_group, at):
                for step in order:
                    if step[0] == "k":
                        _, j, half = step
                        act.wait_ge(s["kT_psum"], at["k"] + 1)
                        copy(k_turned(parity(turned_group), slice(0, KM), j, half * HALF * P, HALF * P),
                             bank[7][0:KM, :].bitcast(BF16)).then_inc(s["kT_ready"], 1)
                    elif step[0] == "st":
                        _, group, c, kb, pair = step
                        width = min(CH, CH - (kb - TPC * c) * P)
                        v = at.here["st"]
                        act.wait_ge(s["st_done"], at["st"] + 1)
                        if not isinstance(at["pv"], int) or at["pv"] >= 2:
                            act.wait_ge(s["pv_done"], at["pv"] - (v > 1 and not pair))
                        A(PT[v % 4][:, :, 0:width], st2[v % 2][:, :, 0:width], ACT.Exp).then_inc(s["exp_done"], 1)
                    elif step[0] == "v4":
                        act.wait_ge(s["pv_done"], at["pv"])
                        take_v(turned_group)
                    at.passed(step)

            take_v(0)
            attend(first, 0, Place())
            with act.Fori(0, 2) as g:
                attend(body, g + 1, Place((first, 1), (body, g)))

            def gate(n, b, early=False):
                act.wait_ge(s["gu_done"], n + 1)
                if not early:
                    act.wait_ge(s["exp_h_ready"], n - 1)
                A(eth[b][:, :], bank[2 + b][:, 0:INTER], ACT.Tanh, scale=0.5).then_inc(s["gate_ready"], 1)

            def turn(n, b, early=False):
                act.wait_ge(s["exp_hT_psum"], n + 1)
                if not early:
                    act.wait_ge(s["y_done"], n - 1)
                copy(ehT[b][:, :], bank[4 + b][:, 0:P]).then_inc(s["exp_hT_ready"], 1)

            def keep_y(n, slot4):
                act.wait_ge(s["y_done"], n + 1)
                act.wait_ge(s["ysb_free"], n + 1)
                copy(ysb[slot4][:, :], bank[6 + slot4 % 2][:, 0:D]).then_inc(s["y_read"], 1)

            gate(0, 0, True)
            gate(1, 1, True)
            turn(0, 0, True)
            gate(2, 0)
            turn(1, 1, True)
            keep_y(0, 0)
            with act.Fori(1, SLOT_TILES // 4) as i:
                for b in range(4):
                    n = 4 * i + b
                    gate(n - 1, (b - 1) % 2)
                    turn(n - 2, b % 2)
                    m = (b - 3) % 4
                    act.wait_ge(s["y_done"], n - 2)
                    act.wait_ge(s["ysb_free"], n - 2)
                    copy(ysb[m][:, :], bank[6 + m % 2][:, 0:D]).then_inc(s["y_read"], 1)
            gate(SLOT_TILES - 1, 1)
            turn(SLOT_TILES - 2, 0)
            keep_y(SLOT_TILES - 3, 1)
            turn(SLOT_TILES - 1, 1)
            keep_y(SLOT_TILES - 2, 2)
            keep_y(SLOT_TILES - 1, 3)
            for b in range(4):
                act.wait_ge(y_stored[b], 16 * (SLOT_TILES // 4))

            attend(body, 3, Place((first, 1), (body, 2)))
            attend(last_part, None, Place((first, 1), (body, 3)))

            with act.Fori(0, NT // 2) as i:
                for b in range(2):
                    t = 2 * i + b
                    act.wait_ge(s["otT_psum"], t + 1)
                    act.wait_ge(s["outp_free"], t + 1)
                    copy(otT[b][:, :, :], bank[b][:, 0:D].rearrange("p (c n) -> p c n", n=P)).then_inc(s["otT_ready"], 1)

        @block.vector
        def _(dve):
            V = nc.vector

            def norm(t, b, early=False):
                if not early:
                    dve.wait_ge(s["xT_psum"], t - 1)
                    dve.wait_ge(s["xn_kept"], t - 1)
                row = res[:, bass.ds(t, 1), :].rearrange("p a n -> p (a n)")
                V.tensor_scalar(xnb[b][:, :], row, mv[:, bass.ds(t, 1), 0], rstd[:, bass.ds(t, 1)],
                                ALU.subtract, ALU.mult).then_inc(s["xn_ready"], 1)

            def rope(t, b):
                dve.wait_ge(s["proj_done"], t + 1)
                y = bank[1 + b][:, :]
                ct = cos_sb[:, bass.ds(t, 1), :].rearrange("p a (c d) -> p (a c) d", d=DH)
                sn = sin_sb[:, bass.ds(t, 1), :].rearrange("p a (c d) -> p (a c) d", d=DH)
                for c in range(2):
                    yc = y[:, c * D:(c + 1) * D].rearrange("p (h d) -> p h d", d=DH)
                    V.tensor_tensor(rope_c[:, c * D:(c + 1) * D].rearrange("p (h d) -> p h d", d=DH), yc,
                                    ct[:, c, :].unsqueeze(1).to_broadcast([P, H, DH]), ALU.mult)
                    for odd in range(2):
                        last = V.tensor_tensor(
                            rope_s[:, c * D:(c + 1) * D].rearrange("p (h d) -> p h d", d=DH)[:, :, odd::2],
                            yc[:, :, 1 - odd::2],
                            sn[:, c, odd::2].unsqueeze(1).to_broadcast([P, H, DH // 2]), ALU.mult)
                last.then_inc(s["rope_done"], 1)
                dve.drain()
                V.tensor_tensor(qk_all[:, bass.ds(t, 1), :].rearrange("p a n -> p (a n)"), rope_c[:, :], rope_s[:, :], ALU.add)

            def shared_act(t, b, early):
                dve.wait_ge(s["proj_read"], t + 1)
                if not early:
                    dve.wait_ge(s["hT_psum"], t - 1)
                V.scalar_tensor_tensor(out=hm[b][:, :], in0=th[b][:, :], scalar=1.0, in1=g1[b][:, :],
                                       op0=ALU.add, op1=ALU.mult)
                dve.drain()
                V.scalar_tensor_tensor(out=hb[b][:, :], in0=hm[b][:, :], scalar=0.5, in1=u1[b][:, :],
                                       op0=ALU.mult, op1=ALU.mult).then_inc(s["act_ready"], 1)

            def shared_add(t):
                dve.wait_ge(s["shared_done"], t + 1)
                row = res[:, bass.ds(t, 1), :].rearrange("p a n -> p (a n)")
                V.tensor_tensor(row, row, bank[6][:, 0:D], ALU.add).then_inc(s["shared_added"], 1)

            dve.wait_ge(s["x_in"], 16)
            for t in range(NT):
                V.bn_stats(stat[:, t, :], res[:, t, :])
            dve.drain()
            for t in range(NT):
                V.bn_aggr(mv[:, t, :], stat[:, t, :])
            dve.drain()
            V.tensor_scalar(var[:, :], mv[:, :, 1], EPS, None, ALU.add).then_inc(s["var_ready"], 1)
            dve.wait_ge(s["root_ready"], 1)
            V.reciprocal(rstd[:, :], root[:, :])
            dve.drain()
            V.tensor_tensor(newton[:, :], rstd[:, :], rstd[:, :], ALU.mult)
            dve.drain()
            V.tensor_tensor(newton[:, :], newton[:, :], var[:, :], ALU.mult)
            dve.drain()
            V.tensor_scalar(newton[:, :], newton[:, :], -0.5, 1.5, ALU.mult, ALU.add)
            dve.drain()
            V.tensor_tensor(rstd[:, :], rstd[:, :], newton[:, :], ALU.mult)
            dve.drain()
            norm(0, 0, True)
            norm(1, 1, True)
            dve.wait_ge(s["w_in"], 16 * 8)
            rope(0, 0)
            shared_act(0, 0, True)
            norm(2, 0)
            rope(1, 1)
            shared_act(1, 1, True)
            shared_add(0)
            norm(3, 1)
            with dve.Fori(1, NT // 2 - 1) as i:
                for b in range(2):
                    t = 2 * i + b
                    rope(t, b)
                    shared_act(t, b, False)
                    shared_add(t - 1)
                    norm(t + 2, b)
            for t in (NT - 2, NT - 1):
                rope(t, t % 2)
                shared_act(t, t % 2, False)
                shared_add(t - 1)
            shared_add(NT - 1)
            dve.drain()
            V.memset(mark[:, :], 0.0).then_inc(s["rows_kept"], 1)

            dve.wait_ge(s["sig_exp"], 1)
            dve.wait_ge(s["ident_made"], 1)
            V.tensor_scalar(key[:, :, :], logit[:, :, :], SATURATED, None, ALU.min)
            V.tensor_scalar(sig[:, :, :], sig[:, :, :], 1.0, None, ALU.add)
            dve.drain()
            V.tensor_reduce(gx[:, :, 0:G], key[:, :, :].rearrange("p t (g e) -> p t g e", e=EG), AX.X, ALU.max)
            V.reciprocal(sig[:, :, :], sig[:, :, :])
            dve.drain()
            for t in range(NT):
                V.max(out=top[:, t, :], in_=gx[:, t, :])
            dve.drain()
            for t in range(NT):
                V.match_replace(out=gx[:, t, :], in_to_replace=top[:, t, :], in_values=gx[:, t, :], imm_value=PICKED)
            dve.drain()
            V.tensor_scalar(gx[:, :, 0:G], gx[:, :, 0:G], PICKED, GONE, ALU.not_equal, ALU.mult)
            dve.drain()
            V.tensor_tensor(ex[:, :, 0:E].rearrange("p t (g e) -> p t g e", e=EG),
                            key[:, :, :].rearrange("p t (g e) -> p t g e", e=EG),
                            gx[:, :, 0:G].unsqueeze(3).to_broadcast([P, NT, G, EG]), ALU.add)
            dve.drain()
            for t in range(NT):
                V.max(out=top[:, t, :], in_=ex[:, t, :])
            dve.drain()
            for t in range(NT):
                V.match_replace(out=ex[:, t, :], in_to_replace=top[:, t, :], in_values=ex[:, t, :], imm_value=PICKED)
            dve.drain()
            V.tensor_scalar(pickb[:, :, :], ex[:, :, 0:E], PICKED, None, ALU.is_equal).then_inc(s["pick_ready"], 1)
            V.tensor_scalar(pick[:, :, :], ex[:, :, 0:E], PICKED, None, ALU.is_equal)
            dve.drain()
            V.tensor_tensor(wgt[:, :, :], pick[:, :, :], sig[:, :, :], ALU.mult)
            dve.drain()
            V.tensor_reduce(wsum[:, :], wgt[:, :, :], AX.X, ALU.add)
            dve.drain()
            V.reciprocal(wsum[:, :], wsum[:, :])
            dve.drain()
            V.scalar_tensor_tensor(out=wgt[:, :, :], in0=wgt[:, :, :], scalar=ROUTE_SCALE,
                                   in1=wsum[:, :].unsqueeze(2).to_broadcast([P, NT, E]),
                                   op0=ALU.mult, op1=ALU.mult)
            dve.wait_ge(s["ranks_done"], 1)
            V.tensor_scalar(cnt[:, :], bank[1][:, 0:E], float(P - 1), None, ALU.add)
            dve.drain()
            V.tensor_scalar(cnt[:, :], cnt[:, :], P.bit_length() - 1, None, ALU.arith_shift_right)
            dve.drain()
            V.tensor_scalar(pad[:, :], cnt[:, :], float(P), None, ALU.mult)
            dve.drain()
            V.tensor_tensor_scan(ends[:, :], ones_e[:, :], pad[:, :], 0.0, ALU.mult, ALU.add)
            dve.drain()
            V.tensor_tensor(owner_cmp[:, :], ends[:, :], tile_at[:, 0:1].to_broadcast([P, E]), ALU.is_le)
            V.tensor_tensor(pad[:, :], ends[:, :], pad[:, :], ALU.subtract)
            dve.drain()
            V.tensor_reduce(owner[:, :], owner_cmp[:, :], AX.X, ALU.add)
            V.scalar_tensor_tensor(out=key[:, :, :], in0=bank[0][:, :].rearrange("p (t e) -> p t e", e=E), scalar=1.0,
                                   in1=pad[:, :].unsqueeze(1).to_broadcast([P, NT, E]),
                                   op0=ALU.add, op1=ALU.add)
            dve.drain()
            V.tensor_scalar(owner[:, :], owner[:, :], float(E - 1), None, ALU.min).then_inc(s["owner_ready"], 1)
            V.tensor_tensor(key[:, :, :], key[:, :, :], pick[:, :, :], ALU.mult)
            dve.drain()
            for t in range(NT):
                V.max(out=slot[:, t, :], in_=key[:, t, :])
            dve.drain()
            V.tensor_scalar(slot_i[:, :, :], slot[:, :, 0:TOPK], 1.0, None, ALU.subtract).then_inc(s["slots_ready"], 1)
            for j in range(TOPK):
                V.tensor_tensor(sig[:, :, :], key[:, :, :], slot[:, :, j:j + 1].to_broadcast([P, NT, E]), ALU.is_equal)
                dve.drain()
                V.tensor_tensor(sig[:, :, :], sig[:, :, :], wgt[:, :, :], ALU.mult)
                dve.drain()
                V.tensor_reduce(c6[:, :, j], sig[:, :, :], AX.X, ALU.add)
                dve.drain()
            dve.wait_ge(s["owner_psum"], 1)
            V.tensor_copy(owner_row[0:1, :], bank[1][0:1, 256:256 + P]).then_inc(s["owner_row_ready"], 1)

            def combine(t):
                dve.wait_ge(gathered[t % 2], 16 * TOPK * (t // 2 + 1))
                for j in range(TOPK):
                    dve.drain()
                    last = V.scalar_tensor_tensor(out=res[:, t, :], in0=yg[t % 2][:, j, :], scalar=c6[:, t, j:j + 1],
                                                  in1=res[:, t, :], op0=ALU.mult, op1=ALU.add)
                last.then_inc(s["combined"], 1)

            def attend(order, turned_group, g, at, combined=()):
                every = len(order) // max(1, len(combined))
                for n, step in enumerate(order):
                    if combined and n % every == every // 2 and n // every < len(combined):
                        combine(combined[n // every])
                    if step[0] == "q":
                        _, j, half = step
                        dve.wait_ge(s["mx_done"], at["ring"] + 1)
                        V.tensor_copy(q_turned(parity(turned_group), slice(0, KQ), j, half * HALF * P, HALF * P),
                                      bank[at.here["ring"] % 2][0:KQ, :].bitcast(BF16)).then_inc(s["mx_read"], 1)
                    elif step[0] == "mx":
                        _, c, t, j, p = step
                        w = CH if p < c else (t % TPC + 1) * P
                        dve.wait_ge(s["mx_done"], at["ring"] + 1)
                        V.tensor_reduce(mpart[:, t % TPC, j, p:p + 1], bank[at.here["ring"] % 2][:, 0:w], AX.X,
                                        ALU.max).then_inc(s["mx_read"], 1)
                    elif step[0] == "mc":
                        c = step[1]
                        dve.drain()
                        V.tensor_reduce(mneg[:, :].rearrange("p (t h) -> p t h", h=HG), mpart[:, :, :, 0:c + 1], AX.X, ALU.max)
                        dve.drain()
                        V.tensor_scalar(mcat[:, :, 0], mneg[:, :], -1.0, None, ALU.mult)
                        dve.drain()
                        V.scalar_tensor_tensor(out=mrem[:, :], in0=mneg[:, :], scalar=-1.0, in1=mcat[:, :, 0],
                                               op0=ALU.mult, op1=ALU.subtract)
                        dve.drain()
                        V.tensor_copy(mcat[:, :, 1], mrem[:, :])
                        dve.drain()
                        V.tensor_tensor(mcat[:, :, 2], mrem[:, :], mcat[:, :, 1], ALU.subtract).then_inc(s["mcat_ready"], 1)
                    elif step[0] == "mt":
                        _, c, pair = step
                        dve.wait_ge(s["misc_done"], at["misc"] + 1)
                        for h in range(2):
                            last = V.tensor_copy(q_turned(parity(turned_group), slice(KQ, KM), 2 * pair + h, c * CH, CH),
                                                 bank[7][KQ:KM, :].bitcast(BF16)[:, h * CH:(h + 1) * CH])
                        last.then_inc(s["misc_read"], 1)
                    elif step[0] == "oe":
                        dve.wait_ge(s["pv_done"], at["pv"])
                        V.tensor_copy(oT[:, :], bank[6][:, :]).then_inc(s["o_read"], 1)
                    elif step[0] == "ot":
                        _, group, c = step
                        dve.wait_ge(s["misc_done"], at["misc"] + 1)
                        o4 = bank[7][:, :].rearrange("p (t h v) -> p t h v", t=TPC, h=HG)
                        V.reciprocal(rden[:, :, :], o4[:, :, :, DH])
                        dve.drain()
                        V.tensor_tensor(o_all[:, TPC * c:TPC * (c + 1), bass.ds((g + group) * GW, GW)].rearrange("p t (h d) -> p t h d", d=DH),
                                        o4[:, :, :, 0:DH], rden[:, :, :].unsqueeze(3).to_broadcast([P, TPC, HG, DH]),
                                        ALU.mult).then_inc(s["misc_read"], 1)
                    at.passed(step)

            attend(first, 0, 0, Place())
            with dve.Fori(0, 2) as g:
                attend(body, g + 1, g, Place((first, 1), (body, g)))

            def rows(n, b, early=False):
                dve.wait_ge(s["exp_x_psum"], n + 1)
                if not early:
                    dve.wait_ge(s["gu_done"], n - 1)
                V.tensor_copy(xgT[b][:, :, :], bank[b][:, 0:D].rearrange("p (c n) -> p c n", n=P)).then_inc(s["exp_x_ready"], 1)

            def gated(n, b, early=False):
                dve.wait_ge(s["gate_ready"], n + 1)
                if not early:
                    dve.wait_ge(s["exp_hT_psum"], n - 1)
                V.scalar_tensor_tensor(out=em[b][:, :], in0=eth[b][:, :], scalar=1.0, in1=bank[2 + b][:, 0:INTER],
                                       op0=ALU.add, op1=ALU.mult)
                dve.drain()
                V.scalar_tensor_tensor(out=eh[b][:, :], in0=em[b][:, :], scalar=0.5, in1=bank[2 + b][:, INTER:2 * INTER],
                                       op0=ALU.mult, op1=ALU.mult).then_inc(s["exp_h_ready"], 1)

            rows(0, 0, True)
            rows(1, 1, True)
            gated(0, 0, True)
            rows(2, 0)
            gated(1, 1, True)
            rows(3, 1)
            gated(2, 0)
            with dve.Fori(1, SLOT_TILES // 4) as i:
                for b in range(4):
                    rows(4 * i + b, b % 2)
                    gated(4 * i + b - 1, (b - 1) % 2)
            gated(SLOT_TILES - 1, 1)

            attend(body, 3, 2, Place((first, 1), (body, 2)), range(NT // 2))
            attend(last_part, None, 3, Place((first, 1), (body, 3)), range(NT // 2, NT))
            dve.drain()
            V.memset(mark[:, :], 0.0).then_inc(s["attention_done"], 1)

            dve.sem_inc(s["outp_free"], 2)
            with dve.Fori(0, NT // 2) as i:
                for b in range(2):
                    t = 2 * i + b
                    dve.wait_ge(s["outp_done"], t + 1)
                    row = res[:, bass.ds(t, 1), :].rearrange("p a n -> p (a n)")
                    V.tensor_tensor(row, row, bank[2 + b][:, 0:D], ALU.add).then_inc(s["outp_free"], 1)

        @block.tensor
        def _(pe):
            mm = nc.tensor.matmul

            def turn(dst, src, eye):
                return nc.tensor.transpose(dst, src, eye)

            def proj(t, b, first=False, early=False):
                pe.wait_ge(s["xn_ready"], t + 1)
                for c in range(DC):
                    last = turn(bank[0][:, c * P:(c + 1) * P], xnb[b][:, c * P:(c + 1) * P], ident[:, :])
                last.then_inc(s["xT_psum"], 1)
                pe.wait_ge(s["xT_ready"], t + 1)
                if not early:
                    pe.wait_ge(s["rope_done"], t - 1)
                if not first:
                    pe.wait_ge(s["proj_read"], t)
                for dst, c0, c1 in ((bank[1 + b], C_QK, C_V), (bank[3 + b], C_V, C_U), (bank[5], C_U, C_END)):
                    for c in range(DC):
                        last = mm(dst[:, 0:c1 - c0], xT[b][:, c, :], wcat[:, c, c0:c1], start=c == 0, stop=c == DC - 1)
                last.then_inc(s["proj_done"], 1)

            def shared(t, b, first=False):
                pe.wait_ge(s["act_ready"], t + 1)
                for c in range(DC):
                    last = turn(bank[7][:, c * P:(c + 1) * P], hb[b][:, c * P:(c + 1) * P], ident[:, :])
                last.then_inc(s["hT_psum"], 1)
                pe.wait_ge(s["hT_ready"], t + 1)
                if not first:
                    pe.wait_ge(s["shared_added"], t)
                for c in range(DC):
                    last = mm(bank[6][:, 0:D], hT[b][:, c, :], sw2[:, c, :], start=c == 0, stop=c == DC - 1)
                last.then_inc(s["shared_done"], 1)

            pe.wait_ge(s["ident_made"], 1)
            pe.wait_ge(s["w_in"], 16 * 8)
            proj(0, 0, True, True)
            proj(1, 1, False, True)
            shared(0, 0, True)
            with pe.Fori(1, NT // 2) as i:
                proj(2 * i, 0)
                shared(2 * i - 1, 1)
                proj(2 * i + 1, 1)
                shared(2 * i, 0)
            shared(NT - 1, 1)

            pe.wait_ge(s["shared_added"], NT)
            pe.wait_ge(s["pick_ready"], 1)
            pk = pickb[:, :, :].rearrange("p t e -> p (t e)")
            mm(bank[0][:, :], triu[:, :], pk, start=True, stop=True, skip_group_check=True)
            for d in range(1, NT):
                mm(bank[0][:, d * E:], onesb[:, :], pk[:, 0:(NT - d) * E], start=False, stop=True, skip_group_check=True)
            for t in range(NT):
                last = mm(bank[1][:, 0:E], onesb[:, :], pickb[:, t, :], start=t == 0, stop=t == NT - 1)
            last.then_inc(s["ranks_done"], 1)
            pe.wait_ge(s["slots_ready"], 1)
            mm(bank[1][0:1, 256:256 + P], owner[:, 0:1], ident[:, :], start=True, stop=True).then_inc(s["owner_psum"], 1)
            pe.wait_ge(s["owner_row_ready"], 1)

            def strips_read(at):
                if not isinstance(at["ring"], int) or at["ring"] > 0:
                    pe.wait_ge(s["mx_read"], at["ring"])

            def misc_free(at):
                if not isinstance(at["misc"], int) or at["misc"] > 0:
                    pe.wait_ge(s["misc_read"], at["misc"])
                if not isinstance(at["k"], int) or at["k"] > 0:
                    pe.wait_ge(s["kT_ready"], at["k"])

            def attend(order, turned_group, g, at):
                for step in order:
                    ring = bank[at.here["ring"] % 2]
                    if step[0] == "q":
                        _, j, half = step
                        if j == 0 and half == 0:
                            pe.wait_ge(s["parts_ready"], turned_group + 1)
                        if not isinstance(at["ring"], int) or at["ring"] >= 2:
                            pe.wait_ge(s["mx_read"], at["ring"] - 1)
                        for k in range(HALF):
                            last = turn(ring[0:KQ, :].bitcast(BF16)[:, k * P:(k + 1) * P], cat[0][:, half * HALF + k, j, :], identb[:, :])
                        last.then_inc(s["mx_done"], 1)
                    elif step[0] == "k":
                        _, j, half = step
                        misc_free(at)
                        for k in range(HALF):
                            last = turn(bank[7][0:KM, :].bitcast(BF16)[:, k * P:(k + 1) * P], cat[1][:, half * HALF + k, j, :], identb[:, :])
                        last.then_inc(s["kT_psum"], 1)
                    elif step[0] == "mx":
                        _, c, t, j, p = step
                        w = CH if p < c else (t % TPC + 1) * P
                        if step == strips(c)[0]:
                            strips_read(at)
                            pe.wait_ge(s["kT_ready"], at["k"])
                            if c == NCH // 2:
                                pe.sem_inc(s["parts_free"], 1)
                        elif not isinstance(at["ring"], int) or at["ring"] >= 2:
                            pe.wait_ge(s["mx_read"], at["ring"] - 1)
                        par = parity(turned_group)
                        last = mm(ring[:, 0:w], q_turned(par, slice(0, KQ), j, t * P, P),
                                  k_turned(par, slice(0, KQ), j, p * CH, w), start=True, stop=p < c)
                        if p == c:
                            last = mm(ring[:, w - P:w], identb[:, :], mask_q[:, :], start=False, stop=True)
                        last.then_inc(s["mx_done"], 1)
                    elif step[0] == "mt":
                        _, c, pair = step
                        misc_free(at)
                        pe.wait_ge(s["mcat_ready"], at["mc"])
                        for j in range(2):
                            for t in range(TPC):
                                k = j * TPC + t
                                last = turn(bank[7][KQ:KM, :].bitcast(BF16)[:, k * P:(k + 1) * P],
                                            mcat[:, t * HG + 2 * pair + j, :], identb[:, :])
                        last.then_inc(s["misc_done"], 1)
                    elif step[0] == "st":
                        _, group, c, kb, pair = step
                        off = max(0, kb - TPC * c) * P
                        v = at.here["st"]
                        if kb == 0 and pair == 0:
                            pe.wait_ge(s["misc_read"], at["misc"])
                        if not isinstance(at["st"], int) or at["st"] >= 2:
                            pe.wait_ge(s["exp_done"], at["st"] - 1)
                        par = parity(g + group)
                        diag = kb >= TPC * c
                        for j in range(2):
                            h = 2 * pair + j
                            last = mm(st2[v % 2][:, j, 0:CH - off], k_turned(par, slice(0, KM), h, kb * P, P),
                                      q_turned(par, slice(0, KM), h, c * CH + off, CH - off), start=True, stop=not diag)
                            if diag:
                                last = mm(st2[v % 2][:, j, 0:P], identb[:, :], mask_k[:, :], start=False, stop=True)
                        last.then_inc(s["st_done"], 1)
                    elif step[0] == "pv":
                        _, group, c, kb = step
                        off = max(0, kb - TPC * c) * P
                        n = at.here["pv"]
                        if kb == 0 and c == 0:
                            pe.wait_ge(s["v4_ready"], at["v4"] + 1)
                        if kb == 0 and (not isinstance(at["oe"], int) or at["oe"] > 0):
                            pe.wait_ge(s["o_read"], at["oe"])
                        pe.wait_ge(s["exp_done"], at["pv"] * 2 + 2)
                        for h in range(HG):
                            last = mm(bank[6][VW * h:VW * (h + 1), off:CH], V4[:, kb, h, :],
                                      PT[(2 * n + h // 2) % 4][:, h % 2, 0:CH - off],
                                      start=kb == 0, stop=kb == TPC * (c + 1) - 1, skip_group_check=True)
                        last.then_inc(s["pv_done"], 1)
                    elif step[0] == "ot":
                        misc_free(at)
                        pe.wait_ge(s["o_read"], at["oe"])
                        for t in range(TPC):
                            last = turn(bank[7][:, t * P:(t + 1) * P], oT[:, t * P:(t + 1) * P], ident[:, :])
                        last.then_inc(s["misc_done"], 1)
                    at.passed(step)
                strips_read(at)
                misc_free(at)
                pe.wait_ge(s["o_read"], at["oe"])

            pe.sem_inc(s["parts_free"], 1)
            attend(first, 0, 0, Place())
            for g in range(2):
                attend(body, g + 1, g, Place((first, 1), (body, g)))

            def rows(n, b, i, early=False):
                pe.wait_ge(tile_in[b], 32 * i + 32)
                if not early:
                    pe.wait_ge(s["exp_x_ready"], n - 1)
                for c in range(DC):
                    last = turn(bank[b % 2][:, c * P:(c + 1) * P], xg[b][:, c * P:(c + 1) * P], ident[:, :])
                last.then_inc(s["exp_x_psum"], 1)

            def gate_up(n, b, early=False):
                pe.wait_ge(s["exp_x_ready"], n + 1)
                if not early:
                    pe.wait_ge(s["exp_h_ready"], n - 1)
                for c in range(DC):
                    last = mm(bank[2 + b % 2][:, 0:2 * INTER], xgT[b % 2][:, c, :], wt[b][:, c * D:(c + 1) * D],
                              start=c == 0, stop=c == DC - 1)
                last.then_inc(s["gu_done"], 1)

            def hidden(n, b, early=False):
                pe.wait_ge(s["exp_h_ready"], n + 1)
                if not early:
                    pe.wait_ge(s["exp_hT_ready"], n - 1)
                turn(bank[4 + b % 2][:, 0:P], eh[b % 2][:, :], ident[:, :]).then_inc(s["exp_hT_psum"], 1)

            def down(n, b, early=False):
                pe.wait_ge(s["exp_hT_ready"], n + 1)
                if not early:
                    pe.wait_ge(s["y_read"], n - 1)
                mm(bank[6 + b % 2][:, 0:D], ehT[b % 2][:, :], wt[b][:, 2 * D:3 * D], start=True, stop=True).then_inc(s["y_done"], 1)

            rows(0, 0, 0, True)
            rows(1, 1, 0, True)
            gate_up(0, 0, True)
            rows(2, 2, 0)
            gate_up(1, 1, True)
            hidden(0, 0, True)
            rows(3, 3, 0)
            gate_up(2, 2)
            hidden(1, 1, True)
            down(0, 0, True)
            for n in range(4, NB):
                rows(n, n, 0)
                gate_up(n - 1, n - 1)
                hidden(n - 2, n - 2)
                down(n - 3, n - 3)
            with pe.Fori(1, SLOT_TILES // NB) as i:
                for b in range(NB):
                    n = NB * i + b
                    rows(n, b, i)
                    gate_up(n - 1, (b - 1) % NB)
                    hidden(n - 2, (b - 2) % NB)
                    down(n - 3, (b - 3) % NB)
            gate_up(SLOT_TILES - 1, NB - 1)
            hidden(SLOT_TILES - 2, NB - 2)
            down(SLOT_TILES - 3, NB - 3)
            hidden(SLOT_TILES - 1, NB - 1)
            down(SLOT_TILES - 2, NB - 2)
            down(SLOT_TILES - 1, NB - 1)
            pe.wait_ge(s["y_read"], SLOT_TILES)

            attend(body, 3, 2, Place((first, 1), (body, 2)))
            attend(last_part, None, 3, Place((first, 1), (body, 3)))

            pe.sem_inc(s["ot_free"], 2)
            with pe.Fori(0, NT // 2) as i:
                for b in range(2):
                    t = 2 * i + b
                    pe.wait_ge(s["ot_ready"], t + 1)
                    pe.wait_ge(s["outp_free"], t + 1)
                    for c in range(DC):
                        last = turn(bank[b][:, c * P:(c + 1) * P], otb[b][:, c * P:(c + 1) * P], ident[:, :])
                    last.then_inc(s["otT_psum"], 1)
                    pe.wait_ge(s["otT_ready"], t + 1)
                    pe.sem_inc(s["ot_free"], 1)
                    for c in range(DC):
                        last = mm(bank[2 + b][:, 0:D], otT[b][:, c, :], wout[:, c, :], start=c == 0, stop=c == DC - 1)
                    last.then_inc(s["outp_done"], 1)
            pe.wait_ge(s["outp_free"], NT + 2)


def rope_tables():
    inv = (np.float32(1.0) / np.float32(10000.0) ** (np.arange(0, DH, 2, dtype=np.float32) / np.float32(DH))).astype(np.float32)
    ang = np.outer(np.arange(T, dtype=np.float32), inv).astype(np.float32)
    ang = np.concatenate([ang, ang], axis=1).astype(np.float64)
    sign = np.where(np.arange(DH) % 2 == 0, -1.0, 1.0)
    c, n = np.cos(ang), np.sin(ang) * sign
    return (np.concatenate([c * ATTN_SCALE, c], 1).astype(np.float32),
            np.concatenate([n * ATTN_SCALE, n], 1).astype(np.float32))


def kernel(L0_attn_x, L0_attn_Wqkv, L0_attn_Wout, L0_ffn_gate_w, L0_ffn_w11, L0_ffn_w33, L0_ffn_w22,
           L0_ffn_sw1, L0_ffn_sw2, L0_ffn_sw3):
    import concourse.bacc as bacc
    from concourse.bass_utils import run_bass_kernel_spmd

    def lay(a):
        return np.ascontiguousarray(a)

    up = np.concatenate([np.asarray(L0_ffn_w11).transpose(0, 2, 1), np.asarray(L0_ffn_w33).transpose(0, 2, 1)], axis=2)
    up = up.reshape(E, DC, P, 2 * INTER).transpose(0, 2, 1, 3).reshape(E, P, DC * 2 * INTER)
    cos, sin = rope_tables()
    arrays = {
        "x": lay(np.asarray(L0_attn_x).reshape(T, D)),
        "wqkvT": lay(np.asarray(L0_attn_Wqkv).T),
        "sw1T": lay(np.asarray(L0_ffn_sw1).T),
        "sw3T": lay(np.asarray(L0_ffn_sw3).T),
        "gateT": lay(np.asarray(L0_ffn_gate_w).T),
        "sw2T": lay(np.asarray(L0_ffn_sw2).T),
        "woutT": lay(np.asarray(L0_attn_Wout).T),
        "wexp": lay(np.concatenate([up, np.asarray(L0_ffn_w22).transpose(0, 2, 1)], axis=2)),
        "cos": cos,
        "sin": sin,
    }
    nc = bacc.Bacc("TRN2", target_bir_lowering=False, num_devices=1)
    args = [nc.dram_tensor(n, a.shape, mybir.dt.from_np(a.dtype), kind="ExternalInput").ap() for n, a in arrays.items()]
    out = nc.dram_tensor("out", [T, D], F32, kind="ExternalOutput").ap()
    layer(nc, *args, out)
    r = run_bass_kernel_spmd(nc, [arrays], core_ids=[0])
    return r.results[0]["out"].reshape(1, T, D)
```

```python
from contextlib import ExitStack

import numpy as np
import concourse.bass as bass
from concourse import mybir

ALU = mybir.AluOpType
ACT = mybir.ActivationFunctionType
AX = mybir.AxisListType
F32 = mybir.dt.float32
BF16 = mybir.dt.bfloat16
I32 = mybir.dt.int32
U32 = mybir.dt.uint32

P = 128
T = 2048
NT = T // P
D = 256
DC = D // P
H = 16
DH = D // H
HG = 4
NG = H // HG
GW = HG * DH
E = 32
INTER = 128
G = 8
EG = E // G
TOPK_G = 4
TOPK = 6
ROUTE_SCALE = 2.5
EPS = 1e-5
SLOT_TILES = T * TOPK // P + E
SLOTS = SLOT_TILES * P
ATTN_SCALE = DH ** -0.5
TERMS = 6
KQ = TERMS * DH
KM = KQ + 3
CH = 512
NCH = T // CH
TPC = CH // P
ZERO_ROWS = 8
QT4 = NT // 4
NB = 8
FT = 4
VW = 32
MASKED = -1e30
SATURATED = 16.6355
GONE = -1e30
SENTINEL = 1e38
PICKED = 2e38

C_QK, C_V, C_G, C_U, C_L = 0, 2 * D, 3 * D, 4 * D, 5 * D
C_END = C_L + E

EARLY, LATE = slice(0, QT4), slice(QT4, NT)
HALF = NT // 2


def strips(c):
    return [("mx", c, t, j, p) for t in range(TPC * c, TPC * c + TPC) for j in range(HG) for p in range(c + 1)]


def turns(half, kinds):
    return [(kind, j, half) for j in range(HG) for kind in kinds]


def blocks(group, c):
    return [(group, c, kb) for kb in range(TPC * (c + 1))]


def weave(pending, key_blocks, fill, goals):
    order, done, later = [], 0, []
    goals = [(0, 0)] + [(4 * block, n) for block, n in goals]
    at = 0

    def some():
        nonlocal done, at
        at += 1
        upto = len(fill)
        for (a0, n0), (a1, n1) in zip(goals, goals[1:]):
            if a0 < at <= a1:
                upto = n0 + -(-(n1 - n0) * (at - a0) // (a1 - a0))
        for step in fill[done:upto]:
            order.append(step)
            if step[0] == "mx" and step == strips(step[1])[-1]:
                order.append(("mc", step[1]))
                later.append((at + 2, ("mt", step[1], 0)))
                later.append((at + 4, ("mt", step[1], 1)))
        done = max(done, upto)
        for when, step in [x for x in later if x[0] <= at]:
            order.append(step)
            later.remove((when, step))

    for group, c, kb in key_blocks:
        order.append(("st", group, c, kb, 0))
        some()
        order.append(("st", group, c, kb, 1))
        some()
        if pending:
            order.append(("pv", *pending))
            if pending[2] == TPC * (pending[1] + 1) - 1:
                order.append(("oe", *pending[:2]))
                later.append((at + 4, ("ot", *pending[:2])))
                if pending[1] == NCH - 1:
                    order.append(("v4",))
        some()
        some()
        pending = (group, c, kb)
    for step in fill[done:]:
        order.append(step)
        if step[0] == "mx" and step == strips(step[1])[-1]:
            order.append(("mc", step[1]))
            later += [(0, ("mt", step[1], 0)), (0, ("mt", step[1], 1))]
    order += [step for _, step in later]
    return order, pending


def projections(tiles):
    order = [("oT", tiles[0])]
    for t in tiles:
        if t + 1 in tiles:
            order.append(("oT", t + 1))
        order.append(("oM", t))
    return order


def flush(order, pending):
    return order + [("pv", *pending), ("oe", *pending[:2]), ("ot", *pending[:2])]


def attention_orders():
    opening = turns(0, ("qs", "ks")) + turns(1, ("qs", "ks"))
    first = strips(0) + [("mc", 0), ("mt", 0, 0), ("mt", 0, 1)]
    fill, goals = [], []
    key_blocks = []
    for c in range(NCH - 1):
        fill += strips(c + 1)
        key_blocks += blocks(0, c)
        goals.append((len(key_blocks) - 1, len(fill)))
    part, pending = weave(None, key_blocks, fill, goals)
    first += part
    early, late = strips(0) + strips(1), turns(1, ("q", "k"))
    mixed = turns(0, ("qs", "kv"))
    for n, step in enumerate(early):
        mixed.append(step)
        if n % 4 == 3 and late:
            mixed.append(late.pop(0))
    key_blocks = blocks(0, NCH - 1) + [b for c in range(NCH - 1) for b in blocks(1, c)]
    fill = mixed + late + strips(2) + strips(3)
    body, ended = weave(None, key_blocks, fill, [(len(key_blocks) - 1, len(fill))])
    ready = NT - TPC
    fill = projections(range(ready))
    last, left = weave(None, blocks(0, NCH - 1), fill, [(len(blocks(0, NCH - 1)) - 1, len(fill))])
    return opening, flush(first, pending), flush(body, ended), flush(last, left) + projections(range(ready, NT))


COUNTED = {"ring": ("mx",), "turn": ("q", "k", "qs", "ks"), "turn_v": ("kv",), "st": ("st",), "pv": ("pv",), "mc": ("mc",), "misc": ("mt", "ot"),
           "oe": ("oe",), "v4": ("v4",)}


class Place:

    def __init__(self, *parts):
        self.base = {name: sum(times * sum(step[0] in kinds for step in order) for order, times in parts)
                     for name, kinds in COUNTED.items()}
        self.here = dict.fromkeys(COUNTED, 0)

    def __getitem__(self, name):
        return self.base[name] + self.here[name]

    def passed(self, step):
        for name, kinds in COUNTED.items():
            self.here[name] += step[0] in kinds


TURN_BANK = {"q": 7, "k": 7, "qs": 0, "ks": 1, "kv": 1}


def parity(group):
    return group % 2


def layer(nc, x, wqkvT, sw1T, sw3T, gateT, sw2T, woutT, wexp, cos, sin, out):
    xg_dram = nc.dram_tensor("gathered_rows", [SLOTS, D], F32, kind="Internal").ap()
    yg_dram = nc.dram_tensor("expert_rows", [SLOTS, D], F32, kind="Internal").ap()
    opening, first, body, last_part = attention_orders()

    with ExitStack() as ctx:
        def sb(name, shape, dt=F32):
            return ctx.enter_context(nc.sbuf_tensor(name, shape, dt))

        def sem(name):
            return ctx.enter_context(nc.semaphore(name))

        bank = [ctx.enter_context(nc.psum_tensor(f"bank{i}", [P, 512], F32)) for i in range(2)]
        st2 = [ctx.enter_context(nc.psum_tensor(f"score_banks{i}", [P, 2, 512], F32)) for i in range(2)]
        bank += [st2[0][:, 0, :], st2[0][:, 1, :], st2[1][:, 0, :], st2[1][:, 1, :]]
        bank += [ctx.enter_context(nc.psum_tensor(f"bank{i}", [P, 512], F32)) for i in (6, 7)]

        def carve(region, words):
            at = 0

            def take(shape, dt=F32):
                nonlocal at
                n = int(np.prod(shape[1:])) * (4 if dt != BF16 else 2) // 4
                part = region[0:shape[0], at:at + n]
                at += n
                assert at <= words
                if dt != F32:
                    part = part.bitcast(dt)
                if len(shape) == 3:
                    part = part.rearrange("p (a b) -> p a b", b=shape[2])
                elif len(shape) == 4:
                    part = part.rearrange("p (a b c) -> p a b c", b=shape[2], c=shape[3])
                return part
            return take

        turned = sb("turned", [P, 2 * HG * T])
        probs = sb("probs", [P, 4 * 2 * CH])
        before = carve(turned[:, 0:HG * T], HG * T)
        routing = carve(turned[:, HG * T:], HG * T)
        ffn = carve(turned[:, HG * T:], HG * T)
        ending = carve(turned[:, 0:HG * T], HG * T)
        before_probs = carve(probs, 4 * 2 * CH)
        ffn_probs = carve(probs, 4 * 2 * CH)

        res = sb("res", [P, NT, D])
        xn_all = sb("xn_all", [P, NT, D])
        qk_all = sb("qk_all", [P, NT, 2 * D])
        v_all = sb("v_all", [P, NT, D])
        o_all = v_all
        ident = sb("ident", [P, P])
        identb = sb("identb", [P, P], BF16)
        wcat = before_probs([P, DC, C_END])
        wout = sb("wout", [P, DC, D])
        sw2 = before_probs([P, DC, D])
        cos_sb = before([P, NT, 2 * DH])
        sin_sb = before([P, NT, 2 * DH])
        stat = before([P, NT, 6])
        mv = sb("mv", [P, NT, 2])
        var = sb("var", [P, NT])
        root = sb("root", [P, NT])
        rstd = sb("rstd", [P, NT])
        newton = sb("newton", [P, NT])
        xnb = [before([P, D]) for b in range(2)]
        xT = [before([P, DC, P]) for b in range(2)]
        rope_c = before([P, 2 * D])
        rope_s = before([P, 2 * D])
        th = [before([P, D]) for b in range(2)]
        g1 = [before([P, D]) for b in range(2)]
        u1 = [before([P, D]) for b in range(2)]
        hm = [before([P, D]) for b in range(2)]
        hb = [before([P, D]) for b in range(2)]
        hT = [before([P, DC, P]) for b in range(2)]
        logit = routing([P, NT, E])
        sig = routing([P, NT, E])
        key = sb("key", [P, NT, E])
        gx = routing([P, NT, G + TOPK_G])
        ex = routing([P, NT, E + 8 - TOPK])
        top = routing([P, NT, 8])
        pick = routing([P, NT, E])
        pickb = routing([P, NT, E], BF16)
        zeros = routing([P, ZERO_ROWS * D])
        wgt = sb("wgt", [P, NT, E])
        wsel = xn_all[:, NT - 2:NT, :].rearrange("p t d -> p (t d)").rearrange("p (t e) -> p t e", e=E)
        wsum = sb("wsum", [P, NT])
        triu = sb("triu", [P, P], BF16)
        onesb = sb("onesb", [P, P], BF16)
        ones_e = sb("ones_e", [P, E])
        cnt = sb("cnt", [P, E], I32)
        pad = sb("pad", [P, E])
        ends = sb("ends", [P, E])
        tile_at = sb("tile_at", [P, 1])
        tile_i = sb("tile_i", [P, 1], I32)
        owner = sb("owner", [P, 1])
        owner_cmp = sb("owner_cmp", [P, E])
        owner_row = sb("owner_row", [1, P], I32)
        ends_row = sb("ends_row", [1, E], I32)
        slot = sb("slot", [P, NT, 8])
        slot_i = sb("slot_i", [P, NT, TOPK], U32)
        c6 = sb("c6", [P, NT, TOPK])
        cat = [sb("cat_q", [P, NT, HG, KQ], BF16), sb("cat_k", [P, NT, HG, KM], BF16)]
        rem = sb("rem", [P, HALF, HG, DH])
        QK = turned[:, :].bitcast(BF16)

        def q_turned(par, rows, j, q0, w):
            return QK[rows, bass.ds(par * 2 * HG * T + j * T + q0, w)]

        def k_turned(par, rows, j, k0, w):
            return QK[rows, bass.ds(par * 2 * HG * T + (HG + j) * T + k0, w)]

        V4 = sb("V4", [P, NT, HG, VW])
        PT = [probs[:, i * 2 * CH:(i + 1) * 2 * CH].rearrange("p (h q) -> p h q", q=CH) for i in range(4)]
        mask_q = sb("mask_q", [P, P], BF16)
        mask_k = sb("mask_k", [P, P], BF16)
        mpart = sb("mpart", [P, TPC, HG, NCH])
        mneg = sb("mneg", [P, TPC * HG])
        mrem = sb("mrem", [P, TPC * HG])
        mcat = sb("mcat", [P, TPC * HG, 3], BF16)
        oT = sb("oT", [P, CH])
        rden = sb("rden", [P, TPC, HG])
        wt = ffn([P, NB, 3 * D])
        xg = [ffn([P, FT, D]) for b in range(2)]
        xgT = [ffn_probs([P, DC, P]) for b in range(2)]
        eth = [ffn_probs([P, INTER]) for b in range(2)]
        em = [ffn_probs([P, INTER]) for b in range(2)]
        eh = [ffn_probs([P, INTER]) for b in range(2)]
        ehT = [ffn_probs([P, P]) for b in range(2)]
        ysb = [ffn_probs([P, FT, D]) for b in range(2)]
        otT = [ending([P, DC, P]) for b in range(2)]
        yg = [xn_all[:, 6 * b:6 * b + 6, :] for b in range(2)]

        names = """x_in w_in tables_in w2_in zeroed ident_made zeros_made
            var_ready root_ready xn_ready xn_kept qk_ready xT_psum xT_ready proj_done rope_done proj_read act_ready hT_psum hT_ready
            shared_done shared_added
            sig_exp pick_ready ranks_done owner_ready owner_psum owner_row_ready plan_ready slots_ready
            parts_ready turn_psum turn_ready turn_psum_v turn_ready_v v4_ready mx_done mx_read
            misc_done misc_read mcat_ready st_done exp_done pv_done o_read
            scattered exp_x_psum exp_x_ready gu_done gate_ready exp_h_ready exp_hT_psum exp_hT_ready
            y_done y_read otT_psum otT_ready outp_done outp_free weights_in combined written""".split()
        s = {n: sem(n) for n in names}
        rows_in = [sem(f"rows_in{b}") for b in range(2)]
        y_stored = [sem(f"y_stored{b}") for b in range(2)]
        gathered = [sem(f"gathered{b}") for b in range(2)]
        block = ctx.enter_context(nc.Block())

        @block.sync
        def _(sp):
            def load_x(tiles):
                sp.dma_start(res[:, tiles, :], x[tiles.start * P:tiles.stop * P, :].rearrange("(t p) d -> p t d", p=P)
                             ).then_inc(s["x_in"], 16)

            load_x(EARLY)
            for dst, src, width in ((C_QK, wqkvT, 3 * D), (C_G, sw1T, D), (C_U, sw3T, D), (C_L, gateT, E)):
                sp.dma_start(wcat[:, :, dst:dst + width],
                             src.rearrange("(c p) n -> p c n", p=P)).then_inc(s["w_in"], 16)
            sp.dma_start(cos_sb[:, :, :], cos.rearrange("(t p) n -> p t n", p=P)).then_inc(s["tables_in"], 16)
            sp.dma_start(sin_sb[:, :, :], sin.rearrange("(t p) n -> p t n", p=P)).then_inc(s["tables_in"], 16)
            sp.wait_ge(s["x_in"], 16)
            load_x(LATE)
            sp.dma_start(sw2[:, :, :], sw2T.rearrange("(c p) n -> p c n", p=P)).then_inc(s["w2_in"], 16)
            sp.dma_start(wout[:, :, :], woutT.rearrange("(c p) n -> p c n", p=P)).then_inc(s["w2_in"], 16)
            sp.wait_ge(s["zeros_made"], 1)
            rows = ZERO_ROWS * P
            for n in range(SLOTS // rows):
                sp.dma_start(xg_dram[n * rows:(n + 1) * rows, :].rearrange("(p r) d -> p (r d)", p=P),
                             zeros[:, :]).then_inc(s["zeroed"], 16)

            def load(e, b, first=False):
                if not first:
                    end = sp.value_load(ends_row[0:1, bass.ds(e - NB, 1)], min_val=1, max_val=SLOT_TILES + 1)
                if not first or b:
                    sp.wait_ge(s["weights_in"], 16 * e)
                if not first:
                    sp.wait_ge(s["y_done"], end)
                    e = sp.snap(e, min_val=0, max_val=E - 1)
                sp.dma_start(wt[:, b, :], wexp[bass.ds(e, 1), :, :].rearrange("e p n -> (e p) n")).then_inc(s["weights_in"], 16)

            sp.wait_ge(s["plan_ready"], 1)
            sp.wait_ge(s["pv_done"], Place((opening, 1), (first, 1), (body, 1))["pv"] + TPC * NCH)
            for b in range(NB):
                load(b, b, True)
            with sp.Fori(1, E // NB) as i:
                for b in range(NB):
                    load(NB * i + b, b)
            for t in range(NT):
                sp.wait_ge(s["outp_free"], t + 1)
                sp.wait_ge(s["combined"], t + 1)
                sp.dma_start(out[t * P:(t + 1) * P, :], res[:, t, :]).then_inc(s["written"], 16)
            sp.wait_ge(s["written"], 16 * NT)

        @block.gpsimd
        def _(gp):
            gp.memset(zeros[:, :], 0.0).then_inc(s["zeros_made"], 1)
            gp.memset(V4[:, :, :, :], 0.0)
            gp.memset(ident[:, :], 0.0)
            gp.memset(identb[:, :], 0.0)
            gp.memset(mask_q[:, :], 0.0)
            gp.memset(mask_k[:, :], 0.0)
            gp.memset(triu[:, :], 1.0)
            gp.memset(onesb[:, :], 1.0)
            gp.memset(ones_e[:, :], 1.0)
            gp.memset(cat[1][:, :, :, KQ:KM], 1.0)
            gp.memset(gx[:, :, G:], SENTINEL)
            gp.memset(ex[:, :, E:], SENTINEL)
            gp.iota(tile_i[:, :], [[0, 1]], base=0, channel_multiplier=P)
            gp.drain()
            gp.memset(V4[:, :, :, DH:DH + 1], 1.0)
            for m in (ident, identb):
                gp.affine_select(out=m[:, :], in_=m[:, :], compare_op=ALU.not_equal, fill=1.0, base=0,
                                 pattern=[[-1, P]], channel_multiplier=1)
            gp.affine_select(out=mask_q[:, :], in_=mask_q[:, :], compare_op=ALU.is_ge, fill=MASKED, base=0,
                             pattern=[[-1, P]], channel_multiplier=1)
            gp.affine_select(out=mask_k[:, :], in_=mask_k[:, :], compare_op=ALU.is_ge, fill=MASKED, base=0,
                             pattern=[[1, P]], channel_multiplier=-1)
            gp.affine_select(out=triu[:, :], in_=triu[:, :], compare_op=ALU.is_gt, fill=0.0, base=0,
                             pattern=[[1, P]], channel_multiplier=-1)
            gp.tensor_copy(tile_at[:, :], tile_i[:, :]).then_inc(s["ident_made"], 1)

            places = (((0, 1, 4), (2, 3), 5), ((0, 2, 5), (1, 3), 4))
            def prepare(g, tiles, signal=True):
                left = rem[:, 0:tiles.stop - tiles.start, :, :]
                for c, (his, mids, lo) in zip(range(2), places):
                    src = qk_all[:, tiles, bass.ds(g * GW + c * D, GW)].rearrange("p t (h d) -> p t h d", d=DH)

                    def part(n):
                        return cat[c][:, tiles, :, n * DH:(n + 1) * DH]

                    for n in his:
                        gp.tensor_copy(part(n), src)
                    gp.drain()
                    gp.tensor_tensor(left, src, part(his[0]), ALU.subtract)
                    gp.drain()
                    for n in mids:
                        gp.tensor_copy(part(n), left)
                    gp.drain()
                    last = gp.tensor_tensor(part(lo), left, part(mids[0]), ALU.subtract)
                    gp.drain()
                if signal:
                    last.then_inc(s["parts_ready"], 1)

            for quarter in range(4):
                gp.wait_ge(s["qk_ready"], QT4 * (quarter + 1))
                prepare(0, slice(QT4 * quarter, QT4 * (quarter + 1)), quarter % 2 == 1)
            def prepare_next(g):
                for half in range(2):
                    if g == 1:
                        gp.wait_ge(s["turn_psum"], 2 * HG * (half + 1))
                    elif half == 0:
                        gp.wait_ge(s["turn_psum_v"], Place((opening, 1), (body, g - 2))["turn_v"] + HG)
                    else:
                        gp.wait_ge(s["turn_psum"], Place((opening, 1), (body, g - 1))["turn"])
                    prepare(g, slice(HALF * half, HALF * (half + 1)))

            prepare_next(1)

            def scatter(tiles):
                for t in tiles:
                    for j in range(TOPK):
                        gp.indirect_dma_start(xg_dram, bass.IndirectOffsetOnAxis(ap=slot_i[:, t, j:j + 1], axis=0),
                                              xn_all[:, t, :], None).then_inc(s["scattered"], 16)

            gp.wait_ge(s["slots_ready"], 1)
            gp.wait_ge(s["zeroed"], 16 * (SLOTS // (ZERO_ROWS * P)))
            scatter(range(NT))
            prepare_next(2)
            prepare_next(3)

            with gp.Fori(0, SLOT_TILES // (2 * FT)) as i:
                for h in range(2):
                    k = 2 * i + h
                    gp.wait_ge(s["y_read"], FT * k + FT)
                    gp.dma_start(yg_dram[bass.ds(k * (FT * P), FT * P), :].rearrange("(a p) d -> p a d", p=P),
                                 ysb[h][:, :, :]).then_inc(y_stored[h], 16)
            for h in range(2):
                gp.wait_ge(y_stored[h], 16 * (SLOT_TILES // (2 * FT)))
            for t in range(NT):
                if t >= 2:
                    gp.wait_ge(s["combined"], t - 1)
                for j in range(TOPK):
                    gp.indirect_dma_start(yg[t % 2][:, j, :], None, yg_dram,
                                          bass.IndirectOffsetOnAxis(ap=slot_i[:, t, j:j + 1], axis=0)).then_inc(gathered[t % 2], 16)

        @block.scalar
        def _(act):
            A = nc.scalar.activation

            def copy(dst, src):
                return A(dst, src, ACT.Copy)

            def row_turned(t, b, early=False):
                act.wait_ge(s["xT_psum"], t + 1)
                copy(xn_all[:, bass.ds(t, 1), :].rearrange("p a n -> p (a n)"), xnb[b][:, :]).then_inc(s["xn_kept"], 1)
                if not early:
                    act.wait_ge(s["proj_done"], t - 1)
                copy(xT[b][:, :, :], bank[0][:, 0:D].rearrange("p (c n) -> p c n", n=P)).then_inc(s["xT_ready"], 1)

            def proj_read(t, b, early=False):
                act.wait_ge(s["proj_done"], t + 1)
                if not early:
                    act.wait_ge(s["act_ready"], t - 1)
                A(th[b][:, :], bank[3 + b][:, D:2 * D], ACT.Tanh, scale=0.5)
                copy(g1[b][:, :], bank[3 + b][:, D:2 * D])
                copy(v_all[:, bass.ds(t, 1), :].rearrange("p a n -> p (a n)"), bank[3 + b][:, 0:D])
                copy(u1[b][:, :], bank[5][:, 0:D])
                copy(logit[:, bass.ds(t, 1), :].rearrange("p a n -> p (a n)"), bank[5][:, D:D + E]).then_inc(s["proj_read"], 1)

            def hidden_turned(t, b, early=False):
                act.wait_ge(s["hT_psum"], t + 1)
                if not early:
                    act.wait_ge(s["shared_done"], t - 1)
                copy(hT[b][:, :, :], bank[7][:, 0:D].rearrange("p (c n) -> p c n", n=P)).then_inc(s["hT_ready"], 1)

            def gate_exp(quarter):
                act.drain()
                A(sig[:, bass.ds(QT4 * quarter, QT4), :], logit[:, bass.ds(QT4 * quarter, QT4), :], ACT.Exp,
                  scale=-1.0).then_inc(s["sig_exp"], 1)

            act.wait_ge(s["var_ready"], 1)
            A(root[:, EARLY], var[:, EARLY], ACT.Sqrt).then_inc(s["root_ready"], 1)
            row_turned(0, 0, True)
            for t in range(QT4):
                row_turned(t + 1, (t + 1) % 2, t + 1 < 2)
                proj_read(t, t % 2, t < 2)
                if t:
                    hidden_turned(t - 1, (t - 1) % 2, t - 1 < 2)
                if t == 1:
                    act.wait_ge(s["var_ready"], 2)
                    A(root[:, LATE], var[:, LATE], ACT.Sqrt).then_inc(s["root_ready"], 1)
            gate_exp(0)
            with act.Fori(1, 3) as quarter:
                for n in range(QT4):
                    t = QT4 * quarter + n
                    row_turned(t + 1, (n + 1) % 2)
                    proj_read(t, n % 2)
                    hidden_turned(t - 1, (n - 1) % 2)
                gate_exp(quarter)
            for t in range(NT - QT4, NT):
                if t + 1 < NT:
                    row_turned(t + 1, (t + 1) % 2)
                proj_read(t, t % 2)
                hidden_turned(t - 1, (t - 1) % 2)
            gate_exp(3)
            hidden_turned(NT - 1, (NT - 1) % 2)

            def take_v(group):
                copy(V4[:, :, :, 0:DH], v_all[:, :, bass.ds(group * GW, GW)].rearrange("p t (h d) -> p t h d", d=DH)
                     ).then_inc(s["v4_ready"], 1)

            def attend(order, turned_group, at):
                for step in order:
                    if step[0] in ("q", "k", "qs", "ks"):
                        kind, j, half = step
                        dst, rows = (q_turned, KQ) if kind[0] == "q" else (k_turned, KM)
                        act.wait_ge(s["turn_psum"], at["turn"] + 1)
                        copy(dst(parity(turned_group), slice(0, rows), j, half * HALF * P, HALF * P),
                             bank[TURN_BANK[kind]][0:rows, :].bitcast(BF16)).then_inc(s["turn_ready"], 1)
                    elif step[0] == "oe":
                        act.wait_ge(s["pv_done"], at["pv"])
                        if not isinstance(at["misc"], int) or at["misc"] > 0:
                            act.wait_ge(s["misc_done"], at["misc"])
                        copy(oT[:, :], bank[6][:, :]).then_inc(s["o_read"], 1)
                    elif step[0] == "st":
                        _, group, c, kb, pair = step
                        width = min(CH, CH - (kb - TPC * c) * P)
                        v = at.here["st"]
                        act.wait_ge(s["st_done"], at["st"] + 1)
                        if not isinstance(at["pv"], int) or at["pv"] >= 2:
                            act.wait_ge(s["pv_done"], at["pv"] - (v > 1 and not pair))
                        A(PT[v % 4][:, :, 0:width], st2[v % 2][:, :, 0:width], ACT.Exp).then_inc(s["exp_done"], 1)
                    elif step[0] == "v4":
                        act.wait_ge(s["pv_done"], at["pv"])
                        take_v(turned_group)
                    at.passed(step)

            attend(opening, 0, Place())
            take_v(0)
            attend(first, 0, Place((opening, 1)))
            with act.Fori(0, 2) as g:
                attend(body, g + 1, Place((opening, 1), (first, 1), (body, g)))

            def gate(n, b, early=False):
                act.wait_ge(s["gu_done"], n + 1)
                if not early:
                    act.wait_ge(s["exp_h_ready"], n - 1)
                A(eth[b][:, :], bank[2 + b][:, 0:INTER], ACT.Tanh, scale=0.5).then_inc(s["gate_ready"], 1)

            def turn(n, b, early=False):
                act.wait_ge(s["exp_hT_psum"], n + 1)
                if not early:
                    act.wait_ge(s["y_done"], n)
                copy(ehT[b][:, :], bank[4 + b][:, 0:P]).then_inc(s["exp_hT_ready"], 1)

            def keep_y(n, b, i, early=False):
                act.wait_ge(s["y_done"], n + 2)
                if b % FT == 0 and not early:
                    act.wait_ge(y_stored[b // FT], 16 * i)
                copy(ysb[b // FT][:, b % FT, :], bank[6 + b % 2][:, 0:D]).then_inc(s["y_read"], 1)

            def load_rows(k, h):
                act.dma_start(xg[h][:, :, :], xg_dram[bass.ds(k * (FT * P), FT * P), :].rearrange("(a p) d -> p a d", p=P)
                              ).then_inc(rows_in[h], 16)

            act.wait_ge(s["scattered"], 16 * NT * TOPK)
            act.wait_ge(s["pv_done"], Place((opening, 1), (first, 1), (body, 2))["pv"])
            load_rows(0, 0)
            load_rows(1, 1)
            for n in range(2 * FT):
                if n >= 1:
                    gate(n - 1, (n - 1) % 2, n < 3)
                if n == FT:
                    act.wait_ge(s["exp_x_psum"], FT)
                    load_rows(2, 0)
                if n >= 2:
                    turn(n - 2, n % 2, n < 4)
                if n >= 3:
                    keep_y(n - 3, n - 3, 0, True)
            with act.Fori(1, SLOT_TILES // (2 * FT) - 1) as i:
                for b in range(2 * FT):
                    n = 2 * FT * i + b
                    gate(n - 1, (b - 1) % 2)
                    if b % FT == 0:
                        act.wait_ge(s["exp_x_psum"], n)
                        load_rows(2 * i + b // FT + 1, 1 - b // FT)
                    turn(n - 2, b % 2)
                    keep_y(n - 3, (b - 3) % (2 * FT), i - (b < 3))
            i = SLOT_TILES // (2 * FT) - 1
            for b in range(2 * FT):
                n = 2 * FT * i + b
                gate(n - 1, (b - 1) % 2)
                if b == 0:
                    act.wait_ge(s["exp_x_psum"], n)
                    load_rows(2 * i + 1, 1)
                turn(n - 2, b % 2)
                keep_y(n - 3, (b - 3) % (2 * FT), i - (b < 3))
            gate(SLOT_TILES - 1, 1)
            turn(SLOT_TILES - 2, 0)
            keep_y(SLOT_TILES - 3, 2 * FT - 3, i)
            turn(SLOT_TILES - 1, 1)
            keep_y(SLOT_TILES - 2, 2 * FT - 2, i)
            keep_y(SLOT_TILES - 1, 2 * FT - 1, i)
            for h in range(2):
                act.wait_ge(y_stored[h], 16 * (SLOT_TILES // (2 * FT)))

            attend(body, 3, Place((opening, 1), (first, 1), (body, 2)))
            attend(last_part, None, Place((opening, 1), (first, 1), (body, 3)))

        @block.vector
        def _(dve):
            V = nc.vector

            def norm(t, b, early=False):
                if not early:
                    dve.wait_ge(s["xT_psum"], t - 1)
                    dve.wait_ge(s["xn_kept"], t - 1)
                row = res[:, bass.ds(t, 1), :].rearrange("p a n -> p (a n)")
                V.tensor_scalar(xnb[b][:, :], row, mv[:, bass.ds(t, 1), 0], rstd[:, bass.ds(t, 1)],
                                ALU.subtract, ALU.mult).then_inc(s["xn_ready"], 1)

            def rope(t, b):
                dve.wait_ge(s["proj_done"], t + 1)
                y = bank[1 + b][:, :]
                ct = cos_sb[:, bass.ds(t, 1), :].rearrange("p a (c d) -> p (a c) d", d=DH)
                sn = sin_sb[:, bass.ds(t, 1), :].rearrange("p a (c d) -> p (a c) d", d=DH)
                for c in range(2):
                    yc = y[:, c * D:(c + 1) * D].rearrange("p (h d) -> p h d", d=DH)
                    V.tensor_tensor(rope_c[:, c * D:(c + 1) * D].rearrange("p (h d) -> p h d", d=DH), yc,
                                    ct[:, c, :].unsqueeze(1).to_broadcast([P, H, DH]), ALU.mult)
                    for odd in range(2):
                        last = V.tensor_tensor(
                            rope_s[:, c * D:(c + 1) * D].rearrange("p (h d) -> p h d", d=DH)[:, :, odd::2],
                            yc[:, :, 1 - odd::2],
                            sn[:, c, odd::2].unsqueeze(1).to_broadcast([P, H, DH // 2]), ALU.mult)
                last.then_inc(s["rope_done"], 1)
                dve.drain()
                V.tensor_tensor(qk_all[:, t, :], rope_c[:, :], rope_s[:, :], ALU.add).then_inc(s["qk_ready"], 1)

            def shared_act(t, b, early):
                dve.wait_ge(s["proj_read"], t + 1)
                if not early:
                    dve.wait_ge(s["hT_psum"], t - 1)
                V.scalar_tensor_tensor(out=hm[b][:, :], in0=th[b][:, :], scalar=1.0, in1=g1[b][:, :],
                                       op0=ALU.add, op1=ALU.mult)
                dve.drain()
                V.scalar_tensor_tensor(out=hb[b][:, :], in0=hm[b][:, :], scalar=0.5, in1=u1[b][:, :],
                                       op0=ALU.mult, op1=ALU.mult).then_inc(s["act_ready"], 1)

            def shared_add(t):
                dve.wait_ge(s["shared_done"], t + 1)
                row = res[:, bass.ds(t, 1), :].rearrange("p a n -> p (a n)")
                V.tensor_tensor(row, row, bank[6][:, 0:D], ALU.add).then_inc(s["shared_added"], 1)

            def statistics(tiles, part):
                dve.wait_ge(s["x_in"], 16 * part)
                for t in range(tiles.start, tiles.stop):
                    V.bn_stats(stat[:, t, :], res[:, t, :])
                dve.drain()
                for t in range(tiles.start, tiles.stop):
                    V.bn_aggr(mv[:, t, :], stat[:, t, :])
                dve.drain()
                V.tensor_scalar(var[:, tiles], mv[:, tiles, 1], EPS, None, ALU.add).then_inc(s["var_ready"], 1)
                dve.wait_ge(s["root_ready"], part)
                V.reciprocal(rstd[:, tiles], root[:, tiles])
                dve.drain()
                V.tensor_tensor(newton[:, tiles], rstd[:, tiles], rstd[:, tiles], ALU.mult)
                dve.drain()
                V.tensor_tensor(newton[:, tiles], newton[:, tiles], var[:, tiles], ALU.mult)
                dve.drain()
                V.tensor_scalar(newton[:, tiles], newton[:, tiles], -0.5, 1.5, ALU.mult, ALU.add)
                dve.drain()
                V.tensor_tensor(rstd[:, tiles], rstd[:, tiles], newton[:, tiles], ALU.mult)
                dve.drain()

            def route(quarter):
                tiles = slice(QT4 * quarter, QT4 * (quarter + 1))
                each = range(QT4 * quarter, QT4 * (quarter + 1))
                dve.wait_ge(s["sig_exp"], quarter + 1)
                V.tensor_scalar(key[:, tiles, :], logit[:, tiles, :], SATURATED, None, ALU.min)
                V.tensor_scalar(sig[:, tiles, :], sig[:, tiles, :], 1.0, None, ALU.add)
                dve.drain()
                V.tensor_reduce(gx[:, tiles, 0:G], key[:, tiles, :].rearrange("p t (g e) -> p t g e", e=EG), AX.X, ALU.max)
                V.reciprocal(sig[:, tiles, :], sig[:, tiles, :])
                dve.drain()
                for t in each:
                    V.max(out=top[:, t, :], in_=gx[:, t, :])
                dve.drain()
                for t in each:
                    V.match_replace(out=gx[:, t, :], in_to_replace=top[:, t, :], in_values=gx[:, t, :], imm_value=PICKED)
                dve.drain()
                V.tensor_scalar(gx[:, tiles, 0:G], gx[:, tiles, 0:G], PICKED, GONE, ALU.not_equal, ALU.mult)
                dve.drain()
                V.tensor_tensor(ex[:, tiles, 0:E].rearrange("p t (g e) -> p t g e", e=EG),
                                key[:, tiles, :].rearrange("p t (g e) -> p t g e", e=EG),
                                gx[:, tiles, 0:G].unsqueeze(3).to_broadcast([P, QT4, G, EG]), ALU.add)
                dve.drain()
                for t in each:
                    V.max(out=top[:, t, :], in_=ex[:, t, :])
                dve.drain()
                for t in each:
                    V.match_replace(out=ex[:, t, :], in_to_replace=top[:, t, :], in_values=ex[:, t, :], imm_value=PICKED)
                dve.drain()
                V.tensor_scalar(pickb[:, tiles, :], ex[:, tiles, 0:E], PICKED, None, ALU.is_equal).then_inc(s["pick_ready"], 1)
                V.tensor_scalar(pick[:, tiles, :], ex[:, tiles, 0:E], PICKED, None, ALU.is_equal)
                dve.drain()
                V.tensor_tensor(wgt[:, tiles, :], pick[:, tiles, :], sig[:, tiles, :], ALU.mult)
                dve.drain()
                V.tensor_reduce(wsum[:, tiles], wgt[:, tiles, :], AX.X, ALU.add)
                dve.drain()
                V.reciprocal(wsum[:, tiles], wsum[:, tiles])
                dve.drain()
                V.scalar_tensor_tensor(out=wgt[:, tiles, :], in0=wgt[:, tiles, :], scalar=ROUTE_SCALE,
                                       in1=wsum[:, tiles].unsqueeze(2).to_broadcast([P, QT4, E]),
                                       op0=ALU.mult, op1=ALU.mult)

            statistics(EARLY, 1)
            dve.wait_ge(s["ident_made"], 1)
            norm(0, 0, True)
            norm(1, 1, True)
            dve.wait_ge(s["tables_in"], 16 * 2)
            for t in range(NT):
                if t + 2 < NT:
                    norm(t + 2, t % 2)
                rope(t, t % 2)
                shared_act(t, t % 2, t < 2)
                if t >= 2:
                    shared_add(t - 2)
                if t == 1:
                    statistics(LATE, 2)
                if t % QT4 == QT4 - 1:
                    route(t // QT4)
            shared_add(NT - 2)
            shared_add(NT - 1)
            dve.drain()
            dve.wait_ge(s["ranks_done"], 1)
            V.tensor_scalar(cnt[:, :], bank[3][:, 0:E], float(P - 1), None, ALU.add)
            dve.drain()
            V.tensor_scalar(cnt[:, :], cnt[:, :], P.bit_length() - 1, None, ALU.arith_shift_right)
            dve.drain()
            V.tensor_scalar(pad[:, :], cnt[:, :], 1.0, float(P), ALU.max, ALU.mult)
            dve.drain()
            V.tensor_tensor_scan(ends[:, :], ones_e[:, :], pad[:, :], 0.0, ALU.mult, ALU.add)
            dve.drain()
            V.tensor_tensor(owner_cmp[:, :], ends[:, :], tile_at[:, 0:1].to_broadcast([P, E]), ALU.is_le)
            V.tensor_tensor(pad[:, :], ends[:, :], pad[:, :], ALU.subtract)
            dve.drain()
            V.tensor_reduce(owner[:, :], owner_cmp[:, :], AX.X, ALU.add)
            V.scalar_tensor_tensor(out=key[:, :, :], in0=bank[2][:, :].rearrange("p (t e) -> p t e", e=E), scalar=1.0,
                                   in1=pad[:, :].unsqueeze(1).to_broadcast([P, NT, E]),
                                   op0=ALU.add, op1=ALU.add)
            dve.drain()
            V.tensor_scalar(owner[:, :], owner[:, :], float(E - 1), None, ALU.min).then_inc(s["owner_ready"], 1)
            V.tensor_tensor(key[:, :, :], key[:, :, :], pick[:, :, :], ALU.mult)
            dve.drain()
            for t in range(NT):
                V.max(out=slot[:, t, :], in_=key[:, t, :])
            dve.drain()
            V.tensor_scalar(slot_i[:, :, :], slot[:, :, 0:TOPK], 1.0, None, ALU.subtract).then_inc(s["slots_ready"], 1)
            dve.wait_ge(s["owner_psum"], 1)
            V.tensor_copy(owner_row[0:1, :], bank[3][0:1, 256:256 + P]).then_inc(s["owner_row_ready"], 1)
            dve.drain()
            V.tensor_scalar(ends_row[0:1, :], ends[0:1, :], 1.0 / P, 1.0, ALU.mult, ALU.add).then_inc(s["plan_ready"], 1)

            def weigh(j):
                V.tensor_tensor(wsel[:, :, :], key[:, :, :], slot[:, :, j:j + 1].to_broadcast([P, NT, E]), ALU.is_equal)
                dve.drain()
                V.tensor_tensor(wsel[:, :, :], wsel[:, :, :], wgt[:, :, :], ALU.mult)
                dve.drain()
                V.tensor_reduce(c6[:, :, j], wsel[:, :, :], AX.X, ALU.add)
                dve.drain()

            def combine(t):
                dve.wait_ge(gathered[t % 2], 16 * TOPK * (t // 2 + 1))
                for j in range(TOPK):
                    dve.drain()
                    last = V.scalar_tensor_tensor(out=res[:, t, :], in0=yg[t % 2][:, j, :], scalar=c6[:, t, j:j + 1],
                                                  in1=res[:, t, :], op0=ALU.mult, op1=ALU.add)
                last.then_inc(s["combined"], 1)

            def attend(order, turned_group, g, at, between=None, items=()):
                every = len(order) // max(1, len(items))
                for n, step in enumerate(order):
                    if items and n % every == every // 2 and n // every < len(items):
                        between(items[n // every])
                    if step[0] == "mx":
                        _, c, t, j, p = step
                        w = CH if p < c else (t % TPC + 1) * P
                        dve.wait_ge(s["mx_done"], at["ring"] + 1)
                        V.tensor_reduce(mpart[:, t % TPC, j, p:p + 1], bank[at.here["ring"] % 2][:, 0:w], AX.X,
                                        ALU.max).then_inc(s["mx_read"], 1)
                    elif step[0] == "kv":
                        _, j, half = step
                        dve.wait_ge(s["turn_psum_v"], at["turn_v"] + 1)
                        V.tensor_copy(k_turned(parity(turned_group), slice(0, KM), j, half * HALF * P, HALF * P),
                                      bank[TURN_BANK["kv"]][0:KM, :].bitcast(BF16)).then_inc(s["turn_ready_v"], 1)
                    elif step[0] == "mc":
                        c = step[1]
                        dve.drain()
                        V.tensor_reduce(mneg[:, :].rearrange("p (t h) -> p t h", h=HG), mpart[:, :, :, 0:c + 1], AX.X, ALU.max)
                        dve.drain()
                        V.tensor_scalar(mcat[:, :, 0], mneg[:, :], -1.0, None, ALU.mult)
                        dve.drain()
                        V.scalar_tensor_tensor(out=mrem[:, :], in0=mneg[:, :], scalar=-1.0, in1=mcat[:, :, 0],
                                               op0=ALU.mult, op1=ALU.subtract)
                        dve.drain()
                        V.tensor_copy(mcat[:, :, 1], mrem[:, :])
                        dve.drain()
                        V.tensor_tensor(mcat[:, :, 2], mrem[:, :], mcat[:, :, 1], ALU.subtract).then_inc(s["mcat_ready"], 1)
                    elif step[0] == "mt":
                        _, c, pair = step
                        dve.wait_ge(s["misc_done"], at["misc"] + 1)
                        for h in range(2):
                            last = V.tensor_copy(q_turned(parity(turned_group), slice(KQ, KM), 2 * pair + h, c * CH, CH),
                                                 bank[7][KQ:KM, :].bitcast(BF16)[:, h * CH:(h + 1) * CH])
                        last.then_inc(s["misc_read"], 1)
                    elif step[0] == "oT":
                        t = step[1]
                        dve.wait_ge(s["otT_psum"], t + 1)
                        if t >= 2:
                            dve.wait_ge(s["outp_done"], t - 1)
                        V.tensor_copy(otT[t % 2][:, :, :], bank[0][:, 0:D].rearrange("p (c n) -> p c n", n=P)
                                      ).then_inc(s["otT_ready"], 1)
                    elif step[0] == "oM":
                        t = step[1]
                        dve.wait_ge(s["outp_done"], t + 1)
                        V.tensor_tensor(res[:, t, :], res[:, t, :], bank[1][:, 0:D], ALU.add).then_inc(s["outp_free"], 1)
                    elif step[0] == "ot":
                        _, group, c = step
                        dve.wait_ge(s["misc_done"], at["misc"] + 1)
                        o4 = bank[7][:, :].rearrange("p (t h v) -> p t h v", t=TPC, h=HG)
                        V.reciprocal(rden[:, :, :], o4[:, :, :, DH])
                        dve.drain()
                        V.tensor_tensor(o_all[:, TPC * c:TPC * (c + 1), bass.ds((g + group) * GW, GW)].rearrange("p t (h d) -> p t h d", d=DH),
                                        o4[:, :, :, 0:DH], rden[:, :, :].unsqueeze(3).to_broadcast([P, TPC, HG, DH]),
                                        ALU.mult).then_inc(s["misc_read"], 1)
                    at.passed(step)

            attend(first, 0, 0, Place((opening, 1)))
            with dve.Fori(0, 2) as g:
                attend(body, g + 1, g, Place((opening, 1), (first, 1), (body, g)))

            def rows(n, b, early=False):
                dve.wait_ge(s["exp_x_psum"], n + 1)
                if not early:
                    dve.wait_ge(s["gu_done"], n - 1)
                V.tensor_copy(xgT[b][:, :, :], bank[b][:, 0:D].rearrange("p (c n) -> p c n", n=P)).then_inc(s["exp_x_ready"], 1)

            def gated(n, b, early=False):
                dve.wait_ge(s["gate_ready"], n + 1)
                if not early:
                    dve.wait_ge(s["exp_hT_psum"], n - 1)
                V.scalar_tensor_tensor(out=em[b][:, :], in0=eth[b][:, :], scalar=1.0, in1=bank[2 + b][:, 0:INTER],
                                       op0=ALU.add, op1=ALU.mult)
                dve.drain()
                V.scalar_tensor_tensor(out=eh[b][:, :], in0=em[b][:, :], scalar=0.5, in1=bank[2 + b][:, INTER:2 * INTER],
                                       op0=ALU.mult, op1=ALU.mult).then_inc(s["exp_h_ready"], 1)

            rows(0, 0, True)
            rows(1, 1, True)
            gated(0, 0, True)
            rows(2, 0)
            gated(1, 1, True)
            rows(3, 1)
            gated(2, 0)
            with dve.Fori(1, SLOT_TILES // 4) as i:
                for b in range(4):
                    rows(4 * i + b, b % 2)
                    gated(4 * i + b - 1, (b - 1) % 2)
            gated(SLOT_TILES - 1, 1)

            for j in range(TOPK):
                weigh(j)
            attend(body, 3, 2, Place((opening, 1), (first, 1), (body, 2)), combine, range(NT // 2))
            attend(last_part, None, 3, Place((opening, 1), (first, 1), (body, 3)), combine, range(NT // 2, NT))
        @block.tensor
        def _(pe):
            mm = nc.tensor.matmul

            def turn(dst, src, eye):
                return nc.tensor.transpose(dst, src, eye)

            def turn_row(t, b, first=False):
                pe.wait_ge(s["xn_ready"], t + 1)
                if not first:
                    pe.wait_ge(s["xT_ready"], t)
                for c in range(DC):
                    last = turn(bank[0][:, c * P:(c + 1) * P], xnb[b][:, c * P:(c + 1) * P], ident[:, :])
                last.then_inc(s["xT_psum"], 1)

            def proj(t, b, first=False, early=False):
                pe.wait_ge(s["xT_ready"], t + 1)
                if not early:
                    pe.wait_ge(s["rope_done"], t - 1)
                    pe.wait_ge(s["proj_read"], t - 1)
                for dst, c0, c1 in ((bank[1 + b], C_QK, C_V), (bank[3 + b], C_V, C_U), (bank[5], C_U, C_END)):
                    if c0 == C_U and not first:
                        pe.wait_ge(s["proj_read"], t)
                    for c in range(DC):
                        last = mm(dst[:, 0:c1 - c0], xT[b][:, c, :], wcat[:, c, c0:c1], start=c == 0, stop=c == DC - 1)
                last.then_inc(s["proj_done"], 1)

            def turn_hidden(t, b, first=False):
                pe.wait_ge(s["act_ready"], t + 1)
                if not first:
                    pe.wait_ge(s["hT_ready"], t)
                for c in range(DC):
                    last = turn(bank[7][:, c * P:(c + 1) * P], hb[b][:, c * P:(c + 1) * P], ident[:, :])
                last.then_inc(s["hT_psum"], 1)

            def shared_down(t, b, first=False):
                pe.wait_ge(s["hT_ready"], t + 1)
                if not first:
                    pe.wait_ge(s["shared_added"], t)
                for c in range(DC):
                    last = mm(bank[6][:, 0:D], hT[b][:, c, :], sw2[:, c, :], start=c == 0, stop=c == DC - 1)
                last.then_inc(s["shared_done"], 1)

            pe.wait_ge(s["ident_made"], 1)
            turn_row(0, 0, True)
            pe.wait_ge(s["w_in"], 16 * 4)
            for t in range(4):
                turn_row(t + 1, (t + 1) % 2)
                proj(t, t % 2, t == 0, t < 2)
                if t == 2:
                    pe.wait_ge(s["w2_in"], 16 * 2)
                if t >= 2:
                    shared_down(t - 2, t % 2, t == 2)
                if t:
                    turn_hidden(t - 1, (t - 1) % 2, t == 1)
            with pe.Fori(2, NT // 2 - 1) as i:
                for b in range(2):
                    t = 2 * i + b
                    turn_row(t + 1, 1 - b)
                    proj(t, b)
                    shared_down(t - 2, b)
                    turn_hidden(t - 1, 1 - b)
            for t in (NT - 2, NT - 1):
                if t + 1 < NT:
                    turn_row(t + 1, (t + 1) % 2)
                proj(t, t % 2)
                shared_down(t - 2, t % 2)
                turn_hidden(t - 1, (t - 1) % 2)
            shared_down(NT - 2, NT % 2)
            turn_hidden(NT - 1, (NT - 1) % 2)
            shared_down(NT - 1, (NT - 1) % 2)

            def strips_read(at):
                if not isinstance(at["ring"], int) or at["ring"] > 0:
                    pe.wait_ge(s["mx_read"], at["ring"])

            def misc_free(at):
                if not isinstance(at["misc"], int) or at["misc"] > 0:
                    pe.wait_ge(s["misc_read"], at["misc"])
                if not isinstance(at["turn"], int) or at["turn"] > 0:
                    pe.wait_ge(s["turn_ready"], at["turn"])

            def attend(order, turned_group, g, at):
                for step in order:
                    ring = bank[at.here["ring"] % 2]
                    if step[0] in TURN_BANK:
                        kind, j, half = step
                        if kind[0] == "q" and j == 0:
                            pe.wait_ge(s["parts_ready"], 2 * turned_group + half + 1)
                        if kind in ("q", "k"):
                            misc_free(at)
                        elif turned_group == 0:
                            if at["turn"] >= 2:
                                pe.wait_ge(s["turn_ready"], at["turn"] - 1)
                        elif kind == "qs":
                            pe.wait_ge(s["turn_ready"], at["turn"])
                        elif kind == "kv" and at["turn_v"]:
                            pe.wait_ge(s["turn_ready_v"], at["turn_v"])
                        rows = KQ if kind[0] == "q" else KM
                        for k in range(HALF):
                            last = turn(bank[TURN_BANK[kind]][0:rows, :].bitcast(BF16)[:, k * P:(k + 1) * P],
                                        cat[kind[0] == "k"][:, half * HALF + k, j, :], identb[:, :])
                        last.then_inc(s["turn_psum_v" if kind == "kv" else "turn_psum"], 1)
                    elif step[0] == "mx":
                        _, c, t, j, p = step
                        w = CH if p < c else (t % TPC + 1) * P
                        if step == strips(c)[0]:
                            strips_read(at)
                            pe.wait_ge(s["turn_ready"], at["turn"])
                            if at["turn_v"]:
                                pe.wait_ge(s["turn_ready_v"], at["turn_v"])
                        elif not isinstance(at["ring"], int) or at["ring"] >= 2:
                            pe.wait_ge(s["mx_read"], at["ring"] - 1)
                        par = parity(turned_group)
                        last = mm(ring[:, 0:w], q_turned(par, slice(0, KQ), j, t * P, P),
                                  k_turned(par, slice(0, KQ), j, p * CH, w), start=True, stop=p < c)
                        if p == c:
                            last = mm(ring[:, w - P:w], identb[:, :], mask_q[:, :], start=False, stop=True)
                        last.then_inc(s["mx_done"], 1)
                    elif step[0] == "mt":
                        _, c, pair = step
                        misc_free(at)
                        pe.wait_ge(s["mcat_ready"], at["mc"])
                        for j in range(2):
                            for t in range(TPC):
                                k = j * TPC + t
                                last = turn(bank[7][KQ:KM, :].bitcast(BF16)[:, k * P:(k + 1) * P],
                                            mcat[:, t * HG + 2 * pair + j, :], identb[:, :])
                        last.then_inc(s["misc_done"], 1)
                    elif step[0] == "st":
                        _, group, c, kb, pair = step
                        off = max(0, kb - TPC * c) * P
                        v = at.here["st"]
                        if kb == 0 and pair == 0:
                            pe.wait_ge(s["misc_read"], at["misc"])
                        if not isinstance(at["st"], int) or at["st"] >= 2:
                            pe.wait_ge(s["exp_done"], at["st"] - 1)
                        par = parity(g + group)
                        diag = kb >= TPC * c
                        for j in range(2):
                            h = 2 * pair + j
                            last = mm(st2[v % 2][:, j, 0:CH - off], k_turned(par, slice(0, KM), h, kb * P, P),
                                      q_turned(par, slice(0, KM), h, c * CH + off, CH - off), start=True, stop=not diag)
                            if diag:
                                last = mm(st2[v % 2][:, j, 0:P], identb[:, :], mask_k[:, :], start=False, stop=True)
                        last.then_inc(s["st_done"], 1)
                    elif step[0] == "pv":
                        _, group, c, kb = step
                        off = max(0, kb - TPC * c) * P
                        n = at.here["pv"]
                        if kb == 0 and c == 0:
                            pe.wait_ge(s["v4_ready"], at["v4"] + 1)
                        if kb == 0 and (not isinstance(at["oe"], int) or at["oe"] > 0):
                            pe.wait_ge(s["o_read"], at["oe"])
                        pe.wait_ge(s["exp_done"], at["pv"] * 2 + 2)
                        for h in range(HG):
                            last = mm(bank[6][VW * h:VW * (h + 1), off:CH], V4[:, kb, h, :],
                                      PT[(2 * n + h // 2) % 4][:, h % 2, 0:CH - off],
                                      start=kb == 0, stop=kb == TPC * (c + 1) - 1, skip_group_check=True)
                        last.then_inc(s["pv_done"], 1)
                    elif step[0] == "ot":
                        misc_free(at)
                        pe.wait_ge(s["o_read"], at["oe"])
                        for t in range(TPC):
                            last = turn(bank[7][:, t * P:(t + 1) * P], oT[:, t * P:(t + 1) * P], ident[:, :])
                        last.then_inc(s["misc_done"], 1)
                    elif step[0] == "oT":
                        t = step[1]
                        if t >= NT - TPC:
                            pe.wait_ge(s["misc_read"], at["misc"])
                        if t:
                            pe.wait_ge(s["otT_ready"], t)
                        for c in range(DC):
                            last = turn(bank[0][:, c * P:(c + 1) * P], o_all[:, t, c * P:(c + 1) * P], ident[:, :])
                        last.then_inc(s["otT_psum"], 1)
                    elif step[0] == "oM":
                        t = step[1]
                        pe.wait_ge(s["otT_ready"], t + 1)
                        if t:
                            pe.wait_ge(s["outp_free"], t)
                        for c in range(DC):
                            last = mm(bank[1][:, 0:D], otT[t % 2][:, c, :], wout[:, c, :], start=c == 0, stop=c == DC - 1)
                        last.then_inc(s["outp_done"], 1)
                    at.passed(step)
                strips_read(at)
                misc_free(at)
                pe.wait_ge(s["o_read"], at["oe"])

            pe.wait_ge(s["pick_ready"], 4)
            pk = pickb[:, :, :].rearrange("p t e -> p (t e)")
            mm(bank[2][:, :], triu[:, :], pk, start=True, stop=True, skip_group_check=True)
            for d in range(1, NT):
                mm(bank[2][:, d * E:], onesb[:, :], pk[:, 0:(NT - d) * E], start=False, stop=True, skip_group_check=True)
            for t in range(NT):
                last = mm(bank[3][:, 0:E], onesb[:, :], pickb[:, t, :], start=t == 0, stop=t == NT - 1)
            last.then_inc(s["ranks_done"], 1)
            pe.wait_ge(s["shared_added"], NT)
            attend(opening, 0, 0, Place())
            pe.wait_ge(s["owner_ready"], 1)
            mm(bank[3][0:1, 256:256 + P], owner[:, 0:1], ident[:, :], start=True, stop=True).then_inc(s["owner_psum"], 1)
            pe.wait_ge(s["owner_row_ready"], 1)

            attend(first, 0, 0, Place((opening, 1)))
            for g in range(2):
                if g == 0:
                    pe.wait_ge(s["slots_ready"], 1)
                    pe.wait_ge(s["zeroed"], 16 * (SLOTS // (ZERO_ROWS * P)))
                attend(body, g + 1, g, Place((opening, 1), (first, 1), (body, g)))

            def rows(n, b, i):
                if b % FT == 0:
                    pe.wait_ge(rows_in[b // FT], 16 * i + 16)
                for c in range(DC):
                    last = turn(bank[b % 2][:, c * P:(c + 1) * P], xg[b // FT][:, b % FT, c * P:(c + 1) * P], ident[:, :])
                last.then_inc(s["exp_x_psum"], 1)

            owners = {}

            def weights(n, key):
                if key not in owners:
                    owners[key] = pe.value_load(owner_row[0:1, bass.ds(n, 1)])
                return owners[key]

            wt_flat = wt[:, :, :].rearrange("p a n -> p (a n)")

            def gate_up(n, b, key=None):
                e = weights(n, key or ("straight", n))
                pe.wait_ge(s["exp_x_ready"], n + 1)
                pe.wait_ge(s["weights_in"], (e & (E - 1)) * 16 + 16)
                at = e % NB * (3 * D)
                for c in range(DC):
                    last = mm(bank[2 + b % 2][:, 0:2 * INTER], xgT[b % 2][:, c, :], wt_flat[:, bass.ds(at + c * D, D)],
                              start=c == 0, stop=c == DC - 1)
                last.then_inc(s["gu_done"], 1)

            def hidden(n, b):
                pe.wait_ge(s["exp_h_ready"], n + 1)
                turn(bank[4 + b % 2][:, 0:P], eh[b % 2][:, :], ident[:, :]).then_inc(s["exp_hT_psum"], 1)

            def down(n, b, early=False, key=None):
                at = weights(n, key or ("straight", n)) % NB * (3 * D)
                pe.wait_ge(s["exp_hT_ready"], n + 1)
                if not early:
                    pe.wait_ge(s["y_read"], n - 1)
                mm(bank[6 + b % 2][:, 0:D], ehT[b % 2][:, :], wt_flat[:, bass.ds(at + 2 * D, D)],
                   start=True, stop=True).then_inc(s["y_done"], 1)

            pe.wait_ge(s["plan_ready"], 1)
            pe.sem_inc(s["y_done"], 1)
            for n in range(2 * FT):
                rows(n, n, 0)
                if n >= 1:
                    gate_up(n - 1, n - 1)
                if n >= 2:
                    hidden(n - 2, n - 2)
                if n >= 3:
                    down(n - 3, n - 3, n < 5)
            with pe.Fori(1, SLOT_TILES // (2 * FT)) as i:
                for b in range(2 * FT):
                    n = 2 * FT * i + b
                    rows(n, b, i)
                    gate_up(n - 1, (b - 1) % (2 * FT), ("loop", b - 1))
                    if b < 2 * FT - 1:
                        weights(n, ("loop", b))
                    hidden(n - 2, (b - 2) % (2 * FT))
                    down(n - 3, (b - 3) % (2 * FT), key=("loop", b - 3))
            gate_up(SLOT_TILES - 1, 1)
            hidden(SLOT_TILES - 2, 0)
            down(SLOT_TILES - 3, 1)
            hidden(SLOT_TILES - 1, 1)
            down(SLOT_TILES - 2, 0)
            down(SLOT_TILES - 1, 1)
            pe.wait_ge(s["y_read"], SLOT_TILES)

            attend(body, 3, 2, Place((opening, 1), (first, 1), (body, 2)))
            attend(last_part, None, 3, Place((opening, 1), (first, 1), (body, 3)))


def rope_tables():
    inv = (np.float32(1.0) / np.float32(10000.0) ** (np.arange(0, DH, 2, dtype=np.float32) / np.float32(DH))).astype(np.float32)
    ang = np.outer(np.arange(T, dtype=np.float32), inv).astype(np.float32)
    ang = np.concatenate([ang, ang], axis=1).astype(np.float64)
    sign = np.where(np.arange(DH) % 2 == 0, -1.0, 1.0)
    c, n = np.cos(ang), np.sin(ang) * sign
    return (np.concatenate([c * ATTN_SCALE, c], 1).astype(np.float32),
            np.concatenate([n * ATTN_SCALE, n], 1).astype(np.float32))


def kernel(L0_attn_x, L0_attn_Wqkv, L0_attn_Wout, L0_ffn_gate_w, L0_ffn_w11, L0_ffn_w33, L0_ffn_w22,
           L0_ffn_sw1, L0_ffn_sw2, L0_ffn_sw3):
    import concourse.bacc as bacc
    from concourse.bass_utils import run_bass_kernel_spmd

    def lay(a):
        return np.ascontiguousarray(a)

    up = np.concatenate([np.asarray(L0_ffn_w11).transpose(0, 2, 1), np.asarray(L0_ffn_w33).transpose(0, 2, 1)], axis=2)
    up = up.reshape(E, DC, P, 2 * INTER).transpose(0, 2, 1, 3).reshape(E, P, DC * 2 * INTER)
    cos, sin = rope_tables()
    arrays = {
        "x": lay(np.asarray(L0_attn_x).reshape(T, D)),
        "wqkvT": lay(np.asarray(L0_attn_Wqkv).T),
        "sw1T": lay(np.asarray(L0_ffn_sw1).T),
        "sw3T": lay(np.asarray(L0_ffn_sw3).T),
        "gateT": lay(np.asarray(L0_ffn_gate_w).T),
        "sw2T": lay(np.asarray(L0_ffn_sw2).T),
        "woutT": lay(np.asarray(L0_attn_Wout).T),
        "wexp": lay(np.concatenate([up, np.asarray(L0_ffn_w22).transpose(0, 2, 1)], axis=2)),
        "cos": cos,
        "sin": sin,
    }
    nc = bacc.Bacc("TRN2", target_bir_lowering=False, num_devices=1)
    args = [nc.dram_tensor(n, a.shape, mybir.dt.from_np(a.dtype), kind="ExternalInput").ap() for n, a in arrays.items()]
    out = nc.dram_tensor("out", [T, D], F32, kind="ExternalOutput").ap()
    layer(nc, *args, out)
    r = run_bass_kernel_spmd(nc, [arrays], core_ids=[0])
    return r.results[0]["out"].reshape(1, T, D)
```
